# Optimizing a Trainium2 kernel written in Bass

```python
import numpy as np
import jax
import jax.numpy as jnp

def _softmax(x, axis=-1):
    return jax.nn.softmax(x, axis=axis)

def _gelu(x):
    return jax.nn.gelu(x, approximate=True)

def _silu(x):
    return jax.nn.silu(x)

def _sigmoid(x):
    return jax.nn.sigmoid(x)

def _layernorm(x, axis=-1, eps=1e-05):
    m = jnp.mean(x, axis=axis, keepdims=True)
    v = jnp.var(x, axis=axis, keepdims=True)
    return (x - m) / jnp.sqrt(v + eps)

def _scatter_add(tgt, idx, src, axis=0):
    return tgt.at[idx].add(src)

def _segment_sum(src, seg, n):
    return jax.ops.segment_sum(src, seg, n)
kernel_name = 'mk_adj_preln_d1_adj_r2_febfc6'

def setup_inputs(seed: int=0):
    np.random.seed(seed)
    _w = jnp.asarray

    def _rec_inputs():
        import jax
        import jax.numpy as jnp
        _gk = jax.random.key(seed)
        x = -0.0005207 + 1.001 * jax.random.normal(jax.random.fold_in(_gk, 1), (4096, 128), jnp.float32)
        _w = (1.0 + jnp.arange(4096, dtype=jnp.float32)) ** (-0.5)
        _w = _w / _w.mean()
        _pij = jnp.clip(0.000976562 * _w[:, None] * _w[None, :], 0.0, 1.0)
        _a = jax.random.uniform(jax.random.fold_in(_gk, 2), (4096, 4096)) < _pij
        _a = jnp.logical_or(_a, jnp.eye(4096, dtype=bool))
        _af = _a.astype(jnp.float32)
        adj = _af
        return (x, adj)
    x, adj = _rec_inputs()

    def _L0_gnn_setup():
        import jax, jax.numpy as jnp
        import numpy as np
        EPS = 1e-08
        NEG = -10000000000.0

        def _l2norm(v):
            n = jnp.sqrt(jnp.sum(v * v, axis=-1, keepdims=True))
            return v / jnp.maximum(n, EPS)
        key = jax.random.key(seed)
        k1, k2, k3 = jax.random.split(key, 3)
        N, M, D = (4096, 4096, 128)
        x = jax.random.normal(k1, (N, D), dtype=jnp.float32)
        y = jax.random.normal(k2, (M, D), dtype=jnp.float32)
        adj = (jax.random.uniform(k3, (N, M)) < 0.02).astype(jnp.float32)
        adj = adj.at[jnp.arange(N), jnp.arange(N) % M].set(1.0)
        return {'x': x, 'y': y, 'adj': adj}
    _L0_gnn_all = _L0_gnn_setup()
    _L0_gnn_in = {k: v for k, v in _L0_gnn_all.items() if k in ('y',)}
    del _L0_gnn_all
    return {'x': x, 'adj': adj, 'L0_gnn_y': _L0_gnn_in['y']}

def reference(x, adj, L0_gnn_y):
    import jax
    import jax.numpy as jnp

    def _L0_gnn_ref(x, y, adj):
        import jax, jax.numpy as jnp
        import numpy as np
        EPS = 1e-08
        NEG = -10000000000.0

        def _l2norm(v):
            n = jnp.sqrt(jnp.sum(v * v, axis=-1, keepdims=True))
            return v / jnp.maximum(n, EPS)
        cos = _l2norm(x) @ _l2norm(y).T
        masked = cos + (1.0 - adj) * NEG
        P = jax.nn.softmax(masked, axis=-1)
        return 0.5 * (P @ y) + 0.5 * x
    h = jnp.maximum(_layernorm(x, axis=-1), 0.0)
    x = x + _L0_gnn_ref(h, L0_gnn_y, adj)
    return x

_drawn_inputs = setup_inputs


def setup_inputs(seed=0):
    import zlib

    import numpy as np

    out = dict(_drawn_inputs(seed))
    spreads = {}
    factors = {}
    for name, (base, spread) in spreads.items():
        noise = np.random.default_rng([zlib.crc32(name.encode()), seed]).standard_normal(out[name].shape)
        drawn = base * np.exp(spread * noise) if base else spread * noise
        out[name] = jnp.asarray(drawn.astype(out[name].dtype))
    for name, factor in factors.items():
        out[name] = (out[name] * factor).astype(out[name].dtype)
    return out
```

```python
from contextlib import ExitStack

import numpy as np
import concourse.bass as bass
from concourse import mybir

P = 128
N = 4096
M = 4096
D = 128
NT = N // P
MT = M // P
CHUNK_TILES = 8
CW = CHUNK_TILES * P
NC = NT // CHUNK_TILES
STEPS = NC * MT
UNROLL = 4
ROUNDS = MT // UNROLL
BANK = 512
ACC_W = D + 1
PER_BANK = BANK // ACC_W
ACC_BANKS = -(-CHUNK_TILES // PER_BANK)
VW = 2 * D + 1
LN_EPS = 1e-5
NORM_EPS = 1e-8
XSCALE = 2.0 ** 14
YSCALE = 2.0 ** 14
PSCALE = 2.0 ** 12


def build(nc, x, y, y_t, adj_t, out):
    f32, f16 = mybir.dt.float32, mybir.dt.float16
    ALU, ACT, AX = mybir.AluOpType, mybir.ActivationFunctionType, mybir.AxisListType

    with ExitStack() as ctx:
        def sb(name, shape, dt=f32):
            return ctx.enter_context(nc.sbuf_tensor(name, shape, dt))

        def sem(name):
            return ctx.enter_context(nc.semaphore(name))

        x_sb = sb("x_sb", [P, NT, D])
        y_sb = sb("y_sb", [P, MT, D])
        yt_sb = sb("yt_sb", [P, M])
        relu_x = sb("relu_x", [P, NT, D])
        x_unit = sb("x_unit", [P, NT, D])
        square = sb("square", [P, D])
        xt_hi = sb("xt_hi", [P, N], f16)
        xt_lo = sb("xt_lo", [P, N], f16)
        yt_hi = sb("yt_hi", [P, M], f16)
        yt_lo = sb("yt_lo", [P, M], f16)
        v = sb("v", [P, MT, VW], f16)
        adj = sb("adj", [P, UNROLL, CW])
        e = sb("e", [P, UNROLL, CW])
        w_hi = sb("w_hi", [P, UNROLL, CW], f16)
        w_lo = sb("w_lo", [P, UNROLL, CW], f16)
        acc = sb("acc", [P, CHUNK_TILES, ACC_W])
        ident = sb("ident", [P, P])
        ones = sb("ones", [P, P])
        ones16 = sb("ones16", [P, P], f16)
        neg_half = sb("neg_half", [P, NT])
        bn = sb("bn", [P, NT, 6])
        moments = sb("moments", [P, NT, 2])
        rstd = sb("rstd", [P, NT])
        half_rstd = sb("half_rstd", [P, NT])
        x_sumsq = sb("x_sumsq", [P, NT])
        x_norm2 = sb("x_norm2", [P, NT])
        x_rnorm = sb("x_rnorm", [P, NT])
        unit_scale = sb("unit_scale", [P, NT])
        y_sumsq = sb("y_sumsq", [P, MT])
        y_rnorm = sb("y_rnorm", [P, MT])
        exp_scale = sb("exp_scale", [P, MT])
        gmax_p = sb("gmax_p", [P, 1])
        gmax_1 = sb("gmax_1", [1, 1])
        gmax = sb("gmax", [P, 1])
        rgmax = sb("rgmax", [P, 1])
        y_scale = sb("y_scale", [P, 1])
        out_scale = sb("out_scale", [P, 1])
        score_scale = sb("score_scale", [P, 1])
        y_total = sb("y_total", [P, ACC_W])
        empty = sb("empty", [P, CHUNK_TILES])
        total = sb("total", [P, CHUNK_TILES])
        weight = sb("weight", [P, CHUNK_TILES])

        scores = [ctx.enter_context(nc.psum_tensor(f"scores{i}", [P, CW], f32)) for i in range(2)]
        sums = [ctx.enter_context(nc.psum_tensor(f"sums{i}", [P, BANK], f32)) for i in range(ACC_BANKS)]
        misc = ctx.enter_context(nc.psum_tensor("misc", [P, BANK], f32))

        x_landed, y_landed, yt_landed = sem("x_landed"), sem("y_landed"), sem("yt_landed")
        adj_landed = [sem(f"adj_landed{u}") for u in range(UNROLL)]
        consts_ready = sem("consts_ready")
        bn_done, moments_done, rstd_done = sem("bn_done"), sem("moments_done"), sem("rstd_done")
        relu_done, sumsq_done, unit_scaled = sem("relu_done"), sem("sumsq_done"), sem("unit_scaled")
        unit_done, turned, xt_hi_done, xt_done = sem("unit_done"), sem("turned"), sem("xt_hi_done"), sem("xt_done")
        finish_chain = sem("finish_chain")
        pool_chain, dve_chain = sem("pool_chain"), sem("dve_chain")
        gmax_step, gmax_moved, gmax_done = sem("gmax_step"), sem("gmax_moved"), sem("gmax_done")
        y_sumsq_done, exp_scale_done = sem("y_sumsq_done"), sem("exp_scale_done")
        yt_done, v_done, total_ready, y_total_done = sem("yt_done"), sem("v_done"), sem("total_ready"), sem("y_total_done")
        scores_ready, exp_ready, masked = sem("scores_ready"), sem("exp_ready"), sem("masked")
        hi_ready, lo_ready = sem("hi_ready"), sem("lo_ready")
        round_summed, acc_copied, finished, out_stored = (sem("round_summed"), sem("acc_copied"), sem("finished"),
                                                           sem("out_stored"))

        block = ctx.enter_context(nc.Block())

        def cols(start, size):
            return bass.ds(start, size)

        def sweep(eng, round_):
            def chunk(c, first_chunk, last_chunk):
                round_(c, 0, True, first_chunk, False)
                with eng.Fori(1, ROUNDS - last_chunk) as r:
                    round_(c, r, False, first_chunk, False)
                if last_chunk:
                    round_(c, ROUNDS - 1, False, first_chunk, True)

            chunk(0, True, False)
            with eng.Fori(1, NC - 1) as c:
                chunk(c, False, False)
            chunk(NC - 1, False, True)

        @block.sync
        def _(sp):
            sp.dma_start(x_sb[:], x).then_inc(x_landed, 16)
            sp.dma_start(y_sb[:], y).then_inc(y_landed, 16)
            sp.dma_start(yt_sb[:], y_t).then_inc(yt_landed, 16)
            for u in range(UNROLL):
                sp.dma_start(adj[:, u, :], adj_t[u]).then_inc(adj_landed[u], 16)
            with sp.Fori(1, STEPS // UNROLL) as r:
                for u in range(UNROLL):
                    sp.wait_ge(masked, UNROLL * r + (u - UNROLL + 1))
                    sp.dma_start(adj[:, u, :], adj_t[cols(UNROLL * r + u, 1)].rearrange("a p w -> (a p) w")
                                 ).then_inc(adj_landed[u], 16)
            sp.wait_ge(out_stored, 16 * NC)

        @block.gpsimd
        def _(pool):
            pool.memset(ident[:], 0.0).then_inc(pool_chain, 1)
            pool.memset(ones[:], 1.0)
            pool.memset(ones16[:], 1.0)
            pool.memset(neg_half[:], -0.5).then_inc(pool_chain, 1)
            pool.memset(v[:, :, D:D + 1], 1.0)
            pool.wait_ge(pool_chain, 2)
            pool.affine_select(out=ident[:], in_=ident[:], compare_op=ALU.not_equal, fill=1.0, base=0,
                               pattern=[[-1, P]], channel_multiplier=1).then_inc(consts_ready, 1)
            pool.wait_ge(moments_done, 1)
            pool.tensor_scalar(rstd[:], moments[:, :, 1], LN_EPS, None, ALU.add).then_inc(pool_chain, 1)
            pool.wait_ge(pool_chain, 3)
            pool.tensor_tensor(rstd[:], rstd[:], neg_half[:], ALU.pow).then_inc(rstd_done, 1)
            pool.wait_ge(rstd_done, 1)
            pool.tensor_scalar(half_rstd[:], rstd[:], 0.5, None, ALU.mult).then_inc(pool_chain, 1)
            pool.wait_ge(sumsq_done, NT)
            pool.tensor_tensor(x_norm2[:], x_sumsq[:], rstd[:], ALU.mult).then_inc(pool_chain, 1)
            pool.wait_ge(pool_chain, 5)
            pool.tensor_tensor(x_norm2[:], x_norm2[:], rstd[:], ALU.mult).then_inc(pool_chain, 1)
            pool.wait_ge(pool_chain, 6)
            pool.tensor_scalar(x_norm2[:], x_norm2[:], NORM_EPS ** 2, None, ALU.max).then_inc(pool_chain, 1)
            pool.wait_ge(pool_chain, 7)
            pool.tensor_tensor(x_rnorm[:], x_norm2[:], neg_half[:], ALU.pow).then_inc(pool_chain, 1)
            pool.wait_ge(pool_chain, 8)
            pool.tensor_tensor(unit_scale[:], x_rnorm[:], rstd[:], ALU.mult).then_inc(pool_chain, 1)
            pool.wait_ge(pool_chain, 9)
            pool.tensor_scalar(unit_scale[:], unit_scale[:], XSCALE, None, ALU.mult).then_inc(unit_scaled, 1)
            pool.wait_ge(y_sumsq_done, MT)
            pool.tensor_scalar(y_rnorm[:], y_sumsq[:], NORM_EPS ** 2, None, ALU.max).then_inc(pool_chain, 1)
            pool.wait_ge(pool_chain, 10)
            pool.tensor_tensor(y_rnorm[:], y_rnorm[:], neg_half[:], ALU.pow).then_inc(pool_chain, 1)
            pool.wait_ge(pool_chain, 11)
            pool.wait_ge(gmax_done, 1)
            pool.tensor_scalar(exp_scale[:], y_rnorm[:], score_scale[:, 0:1], None,
                               ALU.mult).then_inc(exp_scale_done, 1)
            with pool.Fori(0, NC) as c:
                pool.wait_ge(finished, c + 2)
                pool.dma_start(out[:, cols(c * CHUNK_TILES, CHUNK_TILES), :], x_sb[:, cols(c * CHUNK_TILES, CHUNK_TILES), :]).then_inc(out_stored, 16)

        @block.scalar
        def _(act):
            act.wait_ge(y_landed, 16)
            for t in range(MT):
                if t:
                    act.wait_ge(y_sumsq_done, t)
                act.activation(square[:], y_sb[:, t, :], ACT.Square, accum_out=y_sumsq[:, t:t + 1]
                               ).then_inc(y_sumsq_done, 1)
            act.wait_ge(y_sumsq_done, MT)
            act.wait_ge(relu_done, 1)
            for t in range(NT):
                if t:
                    act.wait_ge(sumsq_done, t)
                act.activation(square[:], relu_x[:, t, :], ACT.Square, accum_out=x_sumsq[:, t:t + 1]
                               ).then_inc(sumsq_done, 1)
            for b in range(NT // 4):
                act.wait_ge(turned, b + 1)
                act.copy(xt_hi[:, b * 512:(b + 1) * 512], misc[:]).then_inc(xt_hi_done, 1)
            act.wait_ge(exp_scale_done, 1)

            def evacuate(c):
                act.wait_ge(round_summed, ROUNDS * (c + 1))
                act.wait_ge(finished, c + 1)
                for b in range(ACC_BANKS):
                    j0, j1 = b * PER_BANK, min((b + 1) * PER_BANK, CHUNK_TILES)
                    last = act.copy(acc[:, j0:j1, :], sums[b][:, 0:(j1 - j0) * ACC_W])
                last.then_inc(acc_copied, 1)

            def exp_scores(i, t, u):
                act.wait_ge(scores_ready, i + 1)
                act.activation(e[:, u % UNROLL, :], scores[u % 2][:], ACT.Exp,
                               scale=exp_scale[:, cols(t, 1)]).then_inc(exp_ready, 1)

            def round_(c, r, first_round, first_chunk, last_round):
                for u in range(UNROLL):
                    i = c * MT + (r * UNROLL + u)
                    if not (last_round and u == UNROLL - 1):
                        exp_scores(i + 1, (r * UNROLL + (u + 1)) % MT, u + 1)
                    act.wait_ge(masked, i + 1)
                    act.activation(w_hi[:, u, :], e[:, u, :], ACT.Copy, scale=PSCALE).then_inc(hi_ready, 1)
                    if first_round and u == 0 and not first_chunk:
                        evacuate(c - 1)

            exp_scores(0, 0, 0)
            sweep(act, round_)
            evacuate(NC - 1)

        @block.vector
        def _(dve):
            dve.wait_ge(x_landed, 16)
            for t in range(NT):
                dve.bn_stats(bn[:, t, :], x_sb[:, t, :]).then_inc(bn_done, 1)
            dve.wait_ge(bn_done, NT)
            for t in range(NT):
                last = dve.bn_aggr(moments[:, t, :], bn[:, t, :])
            last.then_inc(moments_done, 1)
            dve.wait_ge(y_landed, 16)
            dve.tensor_reduce(gmax_p[:], y_sb[:].rearrange("p t d -> p (t d)"), AX.X, ALU.max,
                              apply_absolute_value=True).then_inc(gmax_step, 1)
            dve.wait_ge(moments_done, 1)
            for t in range(NT):
                last = dve.tensor_scalar(relu_x[:, t, :], x_sb[:, t, :], moments[:, t, 0:1], 0.0,
                                         ALU.subtract, ALU.max)
            last.then_inc(relu_done, 1)
            dve.wait_ge(gmax_moved, 1)
            dve.tensor_reduce(gmax_1[:], misc[0:1, 0:P], AX.X, ALU.max).then_inc(gmax_step, 1)
            dve.wait_ge(gmax_moved, 2)
            dve.tensor_scalar(gmax[:], misc[:, P:P + 1], 1e-30, None, ALU.max).then_inc(dve_chain, 1)
            dve.wait_ge(dve_chain, 1)
            dve.reciprocal(rgmax[:], gmax[:]).then_inc(dve_chain, 1)
            dve.tensor_scalar(out_scale[:], gmax[:], 0.5 / YSCALE, None, ALU.mult)
            dve.tensor_scalar(score_scale[:], gmax[:], 1.0 / (XSCALE * YSCALE), None, ALU.mult).then_inc(gmax_done, 1)
            dve.wait_ge(dve_chain, 2)
            dve.tensor_scalar(y_scale[:], rgmax[:], YSCALE, None, ALU.mult).then_inc(dve_chain, 1)
            dve.wait_ge(dve_chain, 3)
            dve.wait_ge(yt_landed, 16)
            dve.tensor_scalar(yt_hi[:], yt_sb[:], y_scale[:, 0:1], None, ALU.mult).then_inc(dve_chain, 1)
            dve.tensor_scalar(v[:, :, 0:D], y_sb[:], y_scale[:, 0:1], None, ALU.mult).then_inc(dve_chain, 1)
            dve.wait_ge(dve_chain, 5)
            dve.scalar_tensor_tensor(yt_lo[:], yt_sb[:], y_scale[:, 0:1], yt_hi[:], ALU.mult,
                                     ALU.subtract).then_inc(yt_done, 1)
            dve.scalar_tensor_tensor(v[:, :, D + 1:VW], y_sb[:], y_scale[:, 0:1], v[:, :, 0:D], ALU.mult,
                                     ALU.subtract).then_inc(v_done, 1)
            dve.wait_ge(relu_done, 1)
            dve.wait_ge(unit_scaled, 1)
            for t in range(NT):
                last = dve.tensor_scalar(x_unit[:, t, :], relu_x[:, t, :], unit_scale[:, t:t + 1], None, ALU.mult)
            last.then_inc(unit_done, 1)
            for t in range(NT):
                last = dve.scalar_tensor_tensor(x_sb[:, t, :], relu_x[:, t, :], half_rstd[:, t:t + 1],
                                                x_sb[:, t, :], ALU.mult, ALU.add)
            last.then_inc(finished, 1)
            dve.wait_ge(total_ready, 1)
            dve.tensor_copy(y_total[:], misc[:, 0:ACC_W]).then_inc(y_total_done, 1)
            for b in range(NT // 4):
                dve.wait_ge(xt_hi_done, b + 1)
                dve.tensor_tensor(xt_lo[:, b * 512:(b + 1) * 512], misc[:], xt_hi[:, b * 512:(b + 1) * 512],
                                  ALU.subtract).then_inc(xt_done, 1)

            def mask(i, u, r_adj):
                dve.wait_ge(exp_ready, i + 1)
                dve.wait_ge(adj_landed[u % UNROLL], 16 * (r_adj + 1))
                dve.tensor_tensor(e[:, u % UNROLL, :], adj[:, u % UNROLL, :],
                                  e[:, u % UNROLL, :], ALU.mult).then_inc(masked, 1)

            def finish(c):
                dve.wait_ge(finished, c + 1)
                dve.wait_ge(acc_copied, c + 1)
                done = 3 + 2 + c * 3
                dve.tensor_scalar(empty[:], acc[:, :, D], 0.0, None, ALU.is_equal).then_inc(dve_chain, 1)
                dve.wait_ge(dve_chain, done + 1)
                dve.scalar_tensor_tensor(total[:], empty[:], y_total[:, D:D + 1], acc[:, :, D], ALU.mult,
                                         ALU.add).then_inc(dve_chain, 1)
                dve.wait_ge(dve_chain, done + 2)
                dve.reciprocal(weight[:], total[:]).then_inc(dve_chain, 1)
                for j in range(CHUNK_TILES):
                    last = dve.scalar_tensor_tensor(acc[:, j, 0:D], y_total[:, 0:D], empty[:, j:j + 1], acc[:, j, 0:D],
                                                    ALU.mult, ALU.add)
                dve.wait_ge(dve_chain, done + 3)
                dve.tensor_scalar(weight[:], weight[:], out_scale[:, 0:1], None, ALU.mult).then_inc(finish_chain, 1)
                dve.wait_ge(finish_chain, c + 1)
                for j in range(CHUNK_TILES):
                    rows = x_sb[:, cols(c * CHUNK_TILES + j, 1), :].rearrange("p a d -> p (a d)")
                    last = dve.scalar_tensor_tensor(rows, acc[:, j, 0:D], weight[:, j:j + 1],
                                                    rows, ALU.mult, ALU.add)
                last.then_inc(finished, 1)

            def round_(c, r, first_round, first_chunk, last_round):
                for u in range(UNROLL):
                    i = c * MT + (r * UNROLL + u)
                    if not (last_round and u == UNROLL - 1):
                        mask(i + 1, u + 1, c * ROUNDS + (r + (u + 1) // UNROLL))
                    dve.wait_ge(hi_ready, i + 1)
                    dve.scalar_tensor_tensor(w_lo[:, u, :], e[:, u, :], PSCALE, w_hi[:, u, :], ALU.mult,
                                             ALU.subtract).then_inc(lo_ready, 1)
                    if first_round and u == 1 and not first_chunk:
                        finish(c - 1)

            mask(0, 0, 0)
            sweep(dve, round_)
            finish(NC - 1)

        @block.tensor
        def _(pe):
            pe.wait_ge(consts_ready, 1)
            pe.wait_ge(gmax_step, 1)
            pe.matmul(misc[0:1, 0:P], gmax_p[:], ident[:], start=True, stop=True).then_inc(gmax_moved, 1)
            pe.wait_ge(gmax_step, 2)
            pe.matmul(misc[:, P:P + 1], ones[0:1, :], gmax_1[:], start=True, stop=True).then_inc(gmax_moved, 1)
            pe.wait_ge(v_done, 1)
            pe.wait_ge(gmax_done, 1)
            for t in range(MT):
                pe.matmul(misc[:, 0:ACC_W], ones16[:], v[:, t, 0:ACC_W], start=(t == 0), stop=False)
                last = pe.matmul(misc[:, 0:D], ones16[:], v[:, t, ACC_W:VW], start=False, stop=(t == MT - 1))
            last.then_inc(total_ready, 1)
            pe.wait_ge(unit_done, 1)
            pe.wait_ge(y_total_done, 1)
            for b in range(NT // 4):
                if b:
                    pe.wait_ge(xt_done, b)
                for j in range(4):
                    last = pe.transpose(misc[:, j * P:(j + 1) * P], x_unit[:, 4 * b + j, :], ident[:])
                last.then_inc(turned, 1)
            pe.wait_ge(xt_done, NT // 4)
            pe.wait_ge(yt_done, 1)

            def score(i, u):
                tile = (i % MT) * P
                first = (i // MT) * CW
                s = scores[u % 2]
                for lhs, parts in ((yt_hi, (xt_hi, xt_lo)), (yt_lo, (xt_hi,))):
                    for part in parts:
                        for h in range(CW // BANK):
                            last = pe.matmul(s[:, h * BANK:(h + 1) * BANK], lhs[:, cols(tile, P)],
                                             part[:, cols(first + h * BANK, BANK)],
                                             start=(lhs is yt_hi and part is xt_hi), stop=(lhs is yt_lo))
                last.then_inc(scores_ready, 1)

            def add_values(t, u, first, last_step):
                for j in range(CHUNK_TILES):
                    o = (j % PER_BANK) * ACC_W
                    bank = sums[j // PER_BANK]
                    w = cols(j * P, P)
                    pe.matmul(bank[:, o:o + ACC_W], w_hi[:, u, j * P:(j + 1) * P], v[:, cols(t, 1), 0:ACC_W].rearrange("p a w -> p (a w)"),
                              start=first and j % PER_BANK == 0, stop=False, skip_group_check=True)
                    pe.matmul(bank[:, o:o + D], w_hi[:, u, j * P:(j + 1) * P], v[:, cols(t, 1), ACC_W:VW].rearrange("p a w -> p (a w)"),
                              start=False, stop=False, skip_group_check=True)
                    last = pe.matmul(bank[:, o:o + ACC_W], w_lo[:, u, j * P:(j + 1) * P], v[:, cols(t, 1), 0:ACC_W].rearrange("p a w -> p (a w)"),
                                     start=False, stop=last_step, skip_group_check=True)
                return last

            def round_(c, r, first_round, first_chunk, last_round):
                for u in range(UNROLL):
                    i = c * MT + (r * UNROLL + u)
                    if not (last_round and u >= UNROLL - 2):
                        pe.wait_ge(exp_ready, i + 1)
                        score(i + 2, u)
                    pe.wait_ge(lo_ready, i + 1)
                    if first_round and u == 0 and not first_chunk:
                        pe.wait_ge(acc_copied, c)
                    last = add_values(r * UNROLL + u, u, first_round and u == 0, False)
                    if u == UNROLL - 1:
                        last.then_inc(round_summed, 1)

            score(0, 0)
            score(1, 1)
            sweep(pe, round_)


def kernel(x, adj, L0_gnn_y):
    import concourse.bacc as bacc
    from concourse.bass_utils import run_bass_kernel_spmd

    x, adj, y = np.asarray(x), np.asarray(adj), np.asarray(L0_gnn_y)
    y_rows = y.reshape(P, MT, D)
    arrays = {
        "x": np.ascontiguousarray(x.reshape(P, NT, D)),
        "y": np.ascontiguousarray(y_rows),
        "y_t": np.ascontiguousarray(y_rows.transpose(2, 1, 0).reshape(D, M)),
        "adj_t": np.ascontiguousarray(
            adj.reshape(P, NC, CHUNK_TILES, P, MT).transpose(1, 4, 3, 2, 0).reshape(STEPS, P, CW)),
    }
    nc = bacc.Bacc("TRN2", target_bir_lowering=False, num_devices=1)
    aps = {name: nc.dram_tensor(name, a.shape, mybir.dt.from_np(a.dtype), kind="ExternalInput").ap()
           for name, a in arrays.items()}
    out = nc.dram_tensor("out", (P, NT, D), mybir.dt.float32, kind="ExternalOutput").ap()
    build(nc, aps["x"], aps["y"], aps["y_t"], aps["adj_t"], out)
    result = run_bass_kernel_spmd(nc, [arrays], core_ids=[0])
    return result.results[0]["out"].reshape(N, D)
```

```python
from contextlib import ExitStack

import numpy as np
import concourse.bass as bass
from concourse import mybir

P = 128
N = 4096
M = 4096
D = 128
NT = N // P
MT = M // P
CHUNK_TILES = 8
CW = CHUNK_TILES * P
NC = NT // CHUNK_TILES
STEPS = NC * MT
UNROLL = 4
ROUNDS = MT // UNROLL
BATCHES = MT // UNROLL
BW = UNROLL * P
BANK = 512
ACC_W = D + 1
PER_BANK = BANK // ACC_W
ACC_BANKS = -(-CHUNK_TILES // PER_BANK)
VW = 2 * D + 1
Y_AHEAD = 2
X_AHEAD = CHUNK_TILES + 2
LN_EPS = 1e-5
NORM_EPS = 1e-8
SCALE = 2.0 ** 14
PSCALE = 2.0 ** 12
Y_FLOOR = (NORM_EPS / SCALE) ** 2
X_FLOOR = (NORM_EPS / SCALE) ** 2 / 4
Y_SUMSQ_ACT = 16
X_SUMSQ_DVE = 4


def build(nc, x, y, adj_t, out):
    f32, f16 = mybir.dt.float32, mybir.dt.float16
    ALU, ACT, AX = mybir.AluOpType, mybir.ActivationFunctionType, mybir.AxisListType

    with ExitStack() as ctx:
        def sb(name, shape, dt=f32):
            return ctx.enter_context(nc.sbuf_tensor(name, shape, dt))

        def sem(name):
            return ctx.enter_context(nc.semaphore(name))

        x_sb = sb("x_sb", [P, NT + X_AHEAD - CHUNK_TILES, D])
        y_sb = sb("y_sb", [P, MT, D])
        y_unit0 = sb("y_unit0", [P, Y_AHEAD * UNROLL, D])
        y_unit_b = sb("y_unit_b", [P, UNROLL, D])
        relu0 = sb("relu0", [P, CHUNK_TILES, D])
        unit0 = sb("unit0", [P, CHUNK_TILES, D])
        relu_t = sb("relu_t", [P, D])
        unit_t = sb("unit_t", [P, D])
        act_junk = sb("act_junk", [P, D])
        xt_hi = sb("xt_hi", [P, N + (X_AHEAD - CHUNK_TILES) * P], f16)
        xt_lo = sb("xt_lo", [P, N + (X_AHEAD - CHUNK_TILES) * P], f16)
        yt_hi = sb("yt_hi", [P, M], f16)
        yt_lo = sb("yt_lo", [P, M], f16)
        v = sb("v", [P, MT, VW], f16)
        adj = sb("adj", [P, UNROLL, CW])
        e = sb("e", [P, UNROLL, CW])
        w_hi = sb("w_hi", [P, UNROLL, CW], f16)
        w_lo = sb("w_lo", [P, UNROLL, CW], f16)
        acc = sb("acc", [P, CHUNK_TILES, ACC_W])
        ident = sb("ident", [P, P])
        ones = sb("ones", [P, P])
        neg_half = sb("neg_half", [P, MT])
        bn0 = sb("bn0", [P, CHUNK_TILES, 6])
        moments0 = sb("moments0", [P, CHUNK_TILES, 2])
        var4_0 = sb("var4_0", [P, CHUNK_TILES])
        half_rstd0 = sb("half_rstd0", [P, CHUNK_TILES])
        sumsq0 = sb("sumsq0", [P, CHUNK_TILES])
        floored0 = sb("floored0", [P, CHUNK_TILES])
        unit_scale0 = sb("unit_scale0", [P, CHUNK_TILES])
        bn_t = sb("bn_t", [P, 6])
        moments_t = sb("moments_t", [P, 2])
        var4_t = sb("var4_t", [P, 1])
        half_rstd_t = sb("half_rstd_t", [P, 1])
        sumsq_t = sb("sumsq_t", [P, 1])
        floored_t = sb("floored_t", [P, 1])
        unit_scale_t = sb("unit_scale_t", [P, 1])
        y_sumsq = sb("y_sumsq", [P, MT])
        y_floored = sb("y_floored", [P, MT])
        y_unit_scale = sb("y_unit_scale", [P, MT])
        ymax_p = sb("ymax_p", [P, 1])
        ymax_1 = sb("ymax_1", [1, 1])
        ymax = sb("ymax", [P, 1])
        y_scale = sb("y_scale", [P, 1])
        y_rscale = sb("y_rscale", [P, 1])
        out_scale = sb("out_scale", [P, 1])
        fold = sb("fold", [P, MT // 2, D])
        y_total = sb("y_total", [P, ACC_W])
        empty = sb("empty", [P, CHUNK_TILES])
        total = sb("total", [P, CHUNK_TILES])
        weight = sb("weight", [P, CHUNK_TILES])
        out_weight = sb("out_weight", [P, CHUNK_TILES])

        scores = [ctx.enter_context(nc.psum_tensor(f"scores{i}", [P, CW], f32)) for i in range(2)]
        sums = [ctx.enter_context(nc.psum_tensor(f"sums{i}", [P, BANK], f32)) for i in range(ACC_BANKS)]
        misc = ctx.enter_context(nc.psum_tensor("misc", [P, BANK], f32))

        x_landed, x_rest_landed = sem("x_landed"), sem("x_rest_landed")
        y_landed = [sem(f"y_landed{b}") for b in range(4)]
        adj_landed = [sem(f"adj_landed{u}") for u in range(UNROLL)]
        zeroed, consts_ready, padded = sem("zeroed"), sem("consts_ready"), sem("padded")
        bn0_done, moments0_done, var0_done, half0_done = (sem("bn0_done"), sem("moments0_done"), sem("var0_done"),
                                                          sem("half0_done"))
        relu0_done, sumsq0_dve, sumsq0_act, floored0_done = (sem("relu0_done"), sem("sumsq0_dve"), sem("sumsq0_act"),
                                                             sem("floored0_done"))
        scale0_done, unit0_done, turned0, hi0_done, split0 = (sem("scale0_done"), sem("unit0_done"), sem("turned0"),
                                                              sem("hi0_done"), sem("split0"))
        tile_bn, tile_moments, tile_relu, tile_var = (sem("tile_bn"), sem("tile_moments"), sem("tile_relu"),
                                                      sem("tile_var"))
        tile_half, tile_residual, tile_sumsq, tile_floored = (sem("tile_half"), sem("tile_residual"),
                                                              sem("tile_sumsq"), sem("tile_floored"))
        tile_scale, tile_unit, tile_turned, tile_hi, tile_split = (sem("tile_scale"), sem("tile_unit"),
                                                                   sem("tile_turned"), sem("tile_hi"),
                                                                   sem("tile_split"))
        y_sumsq_act, y_sumsq_dve, y_floor_done, y_scales_done = (sem("y_sumsq_act"), sem("y_sumsq_dve"),
                                                                 sem("y_floor_done"), sem("y_scales_done"))
        ymax_step, ymax_moved, ymax_done, y_scale_done = (sem("ymax_step"), sem("ymax_moved"), sem("ymax_done"),
                                                          sem("y_scale_done"))
        y_rscale_done, folded, total_summed, total_done = (sem("y_rscale_done"), sem("folded"), sem("total_summed"),
                                                           sem("total_done"))
        y_unit_dve, y_unit_pool, y_turned, y_hi_done, y_split = (sem("y_unit_dve"), sem("y_unit_pool"),
                                                                 sem("y_turned"), sem("y_hi_done"), sem("y_split"))
        v_hi_done, v_ready = sem("v_hi_done"), sem("v_ready")
        scores_ready, exp_ready, masked = sem("scores_ready"), sem("exp_ready"), sem("masked")
        hi_ready, lo_ready = sem("hi_ready"), sem("lo_ready")
        round_summed, acc_copied = sem("round_summed"), sem("acc_copied")
        empty_done, total_ready, weight_done, out_weight_done = (sem("empty_done"), sem("total_ready"),
                                                                 sem("weight_done"), sem("out_weight_done"))
        spread_done, finished, out_stored = sem("spread_done"), sem("finished"), sem("out_stored")

        block = ctx.enter_context(nc.Block())

        def cols(start, size):
            return bass.ds(start, size)

        def tile_of(tensor, t):
            return tensor[:, cols(t, 1), :].rearrange("p a d -> p (a d)")

        def batch_of(tensor, b):
            return tensor[:, cols(b * UNROLL, UNROLL), :]

        Y_ROUNDS = BATCHES - Y_AHEAD

        def sweep(eng, round_, y_prepared=None):
            round_(0, 0, first_round=True, first_chunk=True, y_prep=True)
            with eng.Fori(1, Y_ROUNDS) as r:
                round_(0, r, first_chunk=True, y_prep=True)
            if y_prepared:
                y_prepared()
            with eng.Fori(Y_ROUNDS, ROUNDS) as r:
                round_(0, r, first_chunk=True)
            with eng.Fori(1, NC - 1) as c:
                round_(c, 0, first_round=True)
                with eng.Fori(1, ROUNDS) as r:
                    round_(c, r)
            round_(NC - 1, 0, first_round=True, last_chunk=True)
            with eng.Fori(1, ROUNDS - 1) as r:
                round_(NC - 1, r, last_chunk=True)
            round_(NC - 1, ROUNDS - 1, last_chunk=True, last_round=True)

        def begun(n):
            return n - (CHUNK_TILES - 1)

        @block.sync
        def _(sp):
            sp.dma_start(x_sb[:, 0:CHUNK_TILES, :], x[:, 0:CHUNK_TILES, :]).then_inc(x_landed, 16)
            for q in range(4):
                w = MT // 4
                sp.dma_start(y_sb[:, q * w:(q + 1) * w, :], y[:, q * w:(q + 1) * w, :]).then_inc(y_landed[q], 16)
            sp.dma_start(adj[:, 0, :], adj_t[0]).then_inc(adj_landed[0], 16)
            sp.dma_start(x_sb[:, CHUNK_TILES:NT, :], x[:, CHUNK_TILES:NT, :]).then_inc(x_rest_landed, 16)
            for u in range(1, UNROLL):
                sp.dma_start(adj[:, u, :], adj_t[u]).then_inc(adj_landed[u], 16)
            with sp.Fori(1, STEPS // UNROLL) as r:
                for u in range(UNROLL):
                    sp.wait_ge(masked, UNROLL * r + (u - UNROLL + 1))
                    sp.dma_start(adj[:, u, :], adj_t[cols(UNROLL * r + u, 1)].rearrange("a p w -> (a p) w")
                                 ).then_inc(adj_landed[u], 16)
            sp.wait_ge(out_stored, 16 * NC)

        @block.gpsimd
        def _(pool):
            pool.memset(neg_half[:], -0.5).then_inc(consts_ready, 1)
            pool.memset(ident[:], 0.0).then_inc(zeroed, 1)
            pool.memset(ones[:], 1.0).then_inc(consts_ready, 1)
            pool.wait_ge(zeroed, 1)
            pool.affine_select(out=ident[:], in_=ident[:], compare_op=ALU.not_equal, fill=1.0, base=0,
                               pattern=[[-1, P]], channel_multiplier=1).then_inc(consts_ready, 1)
            pool.memset(v[:, :, D:D + 1], 1.0).then_inc(padded, 1)
            pool.memset(y_total[:, D:ACC_W], float(M)).then_inc(padded, 1)
            pool.memset(x_sb[:, NT:, :], 0.0).then_inc(padded, 1)
            pool.wait_ge(consts_ready, 3)
            pool.wait_ge(moments0_done, 1)
            pool.tensor_scalar(var4_0[:], moments0[:, :, 1], LN_EPS, 4.0, ALU.add, ALU.mult).then_inc(var0_done, 1)
            first = Y_AHEAD * UNROLL
            pool.wait_ge(y_sumsq_act, first)
            pool.tensor_scalar(y_floored[:, 0:first], y_sumsq[:, 0:first], Y_FLOOR, None,
                               ALU.max).then_inc(y_floor_done, 1)
            pool.wait_ge(floored0_done, 1)
            pool.tensor_tensor(unit_scale0[:], floored0[:], neg_half[:, 0:CHUNK_TILES], ALU.pow).then_inc(scale0_done, 1)
            pool.wait_ge(y_floor_done, 1)
            pool.tensor_tensor(y_unit_scale[:, 0:first], y_floored[:, 0:first], neg_half[:, 0:first],
                               ALU.pow).then_inc(y_scales_done, 1)
            pool.wait_ge(ymax_done, 1)
            pool.tensor_tensor(y_scale[:], ymax[:], neg_half[:, 0:1], ALU.pow).then_inc(y_scale_done, 1)
            pool.wait_ge(var0_done, 1)
            pool.tensor_tensor(half_rstd0[:], var4_0[:], neg_half[:, 0:CHUNK_TILES], ALU.pow).then_inc(half0_done, 1)

            def tile_scales(n, first):
                pool.wait_ge(tile_var, begun(n))
                if not first:
                    pool.wait_ge(tile_residual, begun(n - 1))
                    pool.wait_ge(tile_unit, begun(n - 1))
                pool.wait_ge(tile_sumsq, begun(n))
                pool.tensor_tensor(half_rstd_t[:], var4_t[:], neg_half[:, 0:1], ALU.pow).then_inc(tile_half, 1)
                pool.tensor_scalar(floored_t[:], var4_t[:], X_FLOOR, sumsq_t[:, 0:1], ALU.mult,
                                   ALU.max).then_inc(tile_floored, 1)
                pool.wait_ge(tile_floored, begun(n))
                pool.tensor_tensor(unit_scale_t[:], floored_t[:], neg_half[:, 0:1], ALU.pow).then_inc(tile_scale, 1)

            def batch_to_unit(b):
                tiles = cols(b * UNROLL, UNROLL)
                pool.tensor_tensor(y_unit_b[:], y_sb[:, tiles, :],
                                   y_unit_scale[:, tiles].unsqueeze(2).to_broadcast([P, UNROLL, D]),
                                   ALU.mult).then_inc(y_unit_pool, 1)

            tile_scales(CHUNK_TILES, True)

            pool.wait_ge(y_sumsq_act, Y_SUMSQ_ACT)
            pool.wait_ge(y_sumsq_dve, MT - Y_SUMSQ_ACT)
            pool.tensor_scalar(y_floored[:, first:], y_sumsq[:, first:], Y_FLOOR, None, ALU.max).then_inc(y_floor_done, 1)
            pool.wait_ge(y_floor_done, 2)
            nxt = first + UNROLL
            pool.tensor_tensor(y_unit_scale[:, first:nxt], y_floored[:, first:nxt], neg_half[:, first:nxt],
                               ALU.pow).then_inc(y_scales_done, 1)
            pool.wait_ge(y_scales_done, 2)
            batch_to_unit(Y_AHEAD)
            pool.tensor_tensor(y_unit_scale[:, nxt:], y_floored[:, nxt:], neg_half[:, nxt:],
                               ALU.pow).then_inc(y_scales_done, 1)
            pool.wait_ge(y_scales_done, 3)
            with pool.Fori(0, Y_ROUNDS - 1) as r:
                tile_scales(r + X_AHEAD - 1, False)
                pool.wait_ge(y_turned, r + Y_AHEAD + 1)
                batch_to_unit(r + Y_AHEAD + 1)
            half = MT // 2
            pool.tensor_tensor(fold[:], y_sb[:, 0:half, :], y_sb[:, half:MT, :], ALU.add).then_inc(folded, 1)
            folds = 1
            while half > 1:
                half //= 2
                pool.wait_ge(folded, folds)
                pool.tensor_tensor(fold[:, 0:half, :], fold[:, 0:half, :], fold[:, half:2 * half, :],
                                   ALU.add).then_inc(folded, 1)
                folds += 1

            def store(c):
                pool.wait_ge(finished, CHUNK_TILES * (c + 1) + 1)
                pool.dma_start(out[:, cols(c * CHUNK_TILES, CHUNK_TILES), :],
                               x_sb[:, cols(c * CHUNK_TILES, CHUNK_TILES), :]).then_inc(out_stored, 16)

            with pool.Fori(Y_ROUNDS - 1, ROUNDS) as r:
                tile_scales(r + X_AHEAD - 1, False)
            with pool.Fori(1, NC - 1) as c:
                with pool.Fori(0, ROUNDS) as r:
                    tile_scales(c * ROUNDS + r + X_AHEAD - 1, False)
                store(c - 1)
            tile_scales(NT + 1, False)
            store(NC - 2)
            store(NC - 1)

        @block.scalar
        def _(act):
            def y_squares(t0, t1):
                for t in range(t0, t1):
                    if t % (MT // 4) == 0:
                        act.wait_ge(y_landed[t // (MT // 4)], 16)
                    act.activation(e[:, t // CHUNK_TILES, t % CHUNK_TILES * D:(t % CHUNK_TILES + 1) * D], y_sb[:, t, :], ACT.Square, scale=1.0 / SCALE,
                                   accum_out=y_sumsq[:, t:t + 1]).then_inc(y_sumsq_act, 1)

            def y_hi(b, src):
                act.wait_ge(y_turned, b + 1)
                act.copy(yt_hi[:, cols(b * BW, BW)], src).then_inc(y_hi_done, 1)

            def v_hi(b):
                act.activation(v[:, cols(b * UNROLL, UNROLL), 0:D], batch_of(y_sb, b), ACT.Copy,
                               scale=y_scale[:, 0:1]).then_inc(v_hi_done, 1)

            def tile_squares(n):
                act.wait_ge(tile_relu, begun(n))
                act.activation(act_junk[:], relu_t[:], ACT.Square, scale=1.0 / SCALE,
                               accum_out=sumsq_t[:]).then_inc(tile_sumsq, 1)

            def tile_to_unit(n, first):
                act.wait_ge(tile_scale, begun(n))
                if not first:
                    act.wait_ge(tile_turned, begun(n - 1))
                act.activation(unit_t[:], relu_t[:], ACT.Copy, scale=unit_scale_t[:, 0:1]).then_inc(tile_unit, 1)

            def tile_high(n):
                act.wait_ge(tile_turned, begun(n))
                act.copy(xt_hi[:, cols(n * P, P)], misc[:, 0:P]).then_inc(tile_hi, 1)

            y_squares(0, UNROLL)
            act.wait_ge(relu0_done, 1)
            for t in range(X_SUMSQ_DVE, CHUNK_TILES):
                act.activation(unit0[:, t, :], relu0[:, t, :], ACT.Square, scale=1.0 / SCALE,
                               accum_out=sumsq0[:, t:t + 1]).then_inc(sumsq0_act, 1)
            y_squares(UNROLL, Y_AHEAD * UNROLL)
            y_squares(Y_AHEAD * UNROLL, Y_SUMSQ_ACT)
            act.wait_ge(turned0, 1)
            act.copy(xt_hi[:, 0:CW], scores[0][:]).then_inc(hi0_done, 1)
            for b in range(Y_AHEAD):
                y_hi(b, sums[b][:])
            tile_squares(CHUNK_TILES)
            act.wait_ge(y_scale_done, 1)
            act.wait_ge(padded, 1)
            for b in range(Y_AHEAD):
                v_hi(b)

            def exp_scores(i, u):
                act.wait_ge(scores_ready, i + 1)
                act.activation(e[:, u % UNROLL, :], scores[u % 2][:], ACT.Exp,
                               scale=1.0 / SCALE ** 2).then_inc(exp_ready, 1)

            def evacuate(c, first):
                act.wait_ge(round_summed, ROUNDS * (c + 1))
                if not first:
                    act.wait_ge(finished, CHUNK_TILES * c + 1)
                for b in range(ACC_BANKS):
                    j0, j1 = b * PER_BANK, min((b + 1) * PER_BANK, CHUNK_TILES)
                    last = act.copy(acc[:, j0:j1, :], sums[b][:, 0:(j1 - j0) * ACC_W])
                last.then_inc(acc_copied, 1)

            def round_(c, r, first_round=False, first_chunk=False, y_prep=False, last_chunk=False, last_round=False):
                k = c * ROUNDS + r
                for u in range(UNROLL):
                    i = c * MT + (r * UNROLL + u)
                    if not (last_round and u == UNROLL - 1):
                        exp_scores(i + 1, u + 1)
                    if first_round and u == 1 and not first_chunk:
                        evacuate(c - 1, False)
                    act.wait_ge(masked, i + 1)
                    act.activation(w_hi[:, u, :], e[:, u, :], ACT.Copy, scale=PSCALE).then_inc(hi_ready, 1)
                    if u == 0 and y_prep:
                        v_hi(r + Y_AHEAD)
                    if u == 1 and y_prep:
                        y_hi(r + Y_AHEAD, misc[:])
                    if u == 1 and not last_chunk:
                        tile_to_unit(k + X_AHEAD - 1, False)
                    if u == 3 and not last_chunk:
                        tile_high(k + X_AHEAD - 1)
                        tile_squares(k + X_AHEAD)

            exp_scores(0, 0)
            tile_to_unit(CHUNK_TILES, True)
            tile_high(CHUNK_TILES)
            tile_squares(CHUNK_TILES + 1)
            sweep(act, round_)
            evacuate(NC - 1, False)

        @block.vector
        def _(dve):
            def y_squares(t0, t1):
                for t in range(t0, t1):
                    if t % (MT // 4) == 0:
                        dve.wait_ge(y_landed[t // (MT // 4)], 16)
                    dve.tensor_tensor_reduce(fold[:, t - Y_SUMSQ_ACT, :], y_sb[:, t, :], y_sb[:, t, :], SCALE ** -2, 0.0, ALU.mult,
                                             ALU.add, y_sumsq[:, t:t + 1]).then_inc(y_sumsq_dve, 1)

            def y_lo(b, src):
                dve.wait_ge(y_hi_done, b + 1)
                dve.tensor_tensor(yt_lo[:, cols(b * BW, BW)], src, yt_hi[:, cols(b * BW, BW)],
                                  ALU.subtract).then_inc(y_split, 1)

            def v_lo(b):
                dve.wait_ge(v_hi_done, b + 1)
                dve.scalar_tensor_tensor(v[:, cols(b * UNROLL, UNROLL), D + 1:VW], batch_of(y_sb, b), y_scale[:, 0:1],
                                         v[:, cols(b * UNROLL, UNROLL), 0:D], ALU.mult,
                                         ALU.subtract).then_inc(v_ready, 1)

            def tile_stats(n):
                dve.bn_stats(bn_t[:], tile_of(x_sb, n)).then_inc(tile_bn, 1)

            def tile_mean():
                dve.bn_aggr(moments_t[:], bn_t[:]).then_inc(tile_moments, 1)

            def tile_clip(n, first):
                dve.wait_ge(tile_moments, begun(n))
                if not first:
                    dve.wait_ge(tile_floored, begun(n - 1))
                dve.tensor_scalar(var4_t[:], moments_t[:, 1:2], LN_EPS, 4.0, ALU.add, ALU.mult).then_inc(tile_var, 1)
                if not first:
                    dve.wait_ge(tile_residual, begun(n - 1))
                    dve.wait_ge(tile_unit, begun(n - 1))
                dve.tensor_scalar(relu_t[:], tile_of(x_sb, n), moments_t[:, 0:1], 0.0, ALU.subtract,
                                  ALU.max).then_inc(tile_relu, 1)

            def tile_add_half(n):
                dve.wait_ge(tile_relu, begun(n))
                dve.wait_ge(tile_half, begun(n))
                dve.scalar_tensor_tensor(tile_of(x_sb, n), relu_t[:], half_rstd_t[:, 0:1], tile_of(x_sb, n),
                                         ALU.mult, ALU.add).then_inc(tile_residual, 1)

            def tile_low(n):
                dve.wait_ge(tile_hi, begun(n))
                dve.tensor_tensor(xt_lo[:, cols(n * P, P)], misc[:, 0:P], xt_hi[:, cols(n * P, P)],
                                  ALU.subtract).then_inc(tile_split, 1)

            dve.wait_ge(x_landed, 16)
            for t in range(CHUNK_TILES):
                dve.bn_stats(bn0[:, t, :], x_sb[:, t, :]).then_inc(bn0_done, 1)
            dve.wait_ge(bn0_done, CHUNK_TILES)
            for t in range(CHUNK_TILES):
                last = dve.bn_aggr(moments0[:, t, :], bn0[:, t, :])
            last.then_inc(moments0_done, 1)
            dve.wait_ge(moments0_done, 1)
            for t in reversed(range(CHUNK_TILES)):
                last = dve.tensor_scalar(relu0[:, t, :], x_sb[:, t, :], moments0[:, t, 0:1], 0.0,
                                         ALU.subtract, ALU.max)
            last.then_inc(relu0_done, 1)
            dve.wait_ge(relu0_done, 1)
            for t in range(X_SUMSQ_DVE):
                last = dve.tensor_tensor_reduce(unit0[:, t, :], relu0[:, t, :], relu0[:, t, :], SCALE ** -2, 0.0,
                                                ALU.mult, ALU.add, sumsq0[:, t:t + 1])
            last.then_inc(sumsq0_dve, 1)
            dve.wait_ge(sumsq0_dve, 1)
            dve.wait_ge(sumsq0_act, CHUNK_TILES - X_SUMSQ_DVE)
            dve.wait_ge(var0_done, 1)
            dve.scalar_tensor_tensor(floored0[:], var4_0[:], X_FLOOR, sumsq0[:], ALU.mult,
                                     ALU.max).then_inc(floored0_done, 1)
            y_squares(Y_SUMSQ_ACT, MT - 8)
            dve.wait_ge(scale0_done, 1)
            for t in range(CHUNK_TILES):
                last = dve.tensor_scalar(unit0[:, t, :], relu0[:, t, :], unit_scale0[:, t:t + 1], None, ALU.mult)
            last.then_inc(unit0_done, 1)
            dve.wait_ge(y_scales_done, 1)
            for t in range(Y_AHEAD * UNROLL):
                last = dve.tensor_scalar(y_unit0[:, t, :], y_sb[:, t, :], y_unit_scale[:, t:t + 1], None, ALU.mult)
                if t % UNROLL == UNROLL - 1:
                    last.then_inc(y_unit_dve, 1)
            y_squares(MT - 8, MT)
            dve.wait_ge(y_sumsq_act, Y_SUMSQ_ACT)
            dve.wait_ge(y_sumsq_dve, MT - Y_SUMSQ_ACT)
            dve.tensor_reduce(ymax_p[:], y_sumsq[:], AX.X, ALU.max).then_inc(ymax_step, 1)
            dve.wait_ge(hi0_done, 1)
            dve.tensor_tensor(xt_lo[:, 0:CW], scores[0][:], xt_hi[:, 0:CW], ALU.subtract).then_inc(split0, 1)
            y_lo(0, sums[0][:])
            y_lo(1, sums[1][:])
            dve.wait_ge(ymax_moved, 1)
            dve.tensor_reduce(ymax_1[:], misc[0:1, 0:P], AX.X, ALU.max).then_inc(ymax_step, 1)
            dve.wait_ge(x_rest_landed, 16)
            tile_stats(CHUNK_TILES)
            dve.wait_ge(tile_bn, 1)
            tile_mean()
            dve.wait_ge(ymax_moved, 2)
            dve.tensor_scalar(ymax[:], misc[:, P:P + 1], Y_FLOOR, None, ALU.max).then_inc(ymax_done, 1)
            tile_clip(CHUNK_TILES, True)
            dve.wait_ge(y_scale_done, 1)
            dve.reciprocal(y_rscale[:], y_scale[:]).then_inc(y_rscale_done, 1)
            dve.wait_ge(y_rscale_done, 1)
            dve.tensor_scalar(out_scale[:], y_rscale[:], 0.5, None, ALU.mult)
            for b in range(Y_AHEAD):
                v_lo(b)
            tile_add_half(CHUNK_TILES)

            def mask(i, u, k):
                dve.wait_ge(exp_ready, i + 1)
                dve.wait_ge(adj_landed[u % UNROLL], 16 * (k + 1))
                dve.tensor_tensor(e[:, u % UNROLL, :], adj[:, u % UNROLL, :], e[:, u % UNROLL, :],
                                  ALU.mult).then_inc(masked, 1)

            def weigh(c):
                dve.wait_ge(acc_copied, c + 1)
                dve.tensor_scalar(empty[:], acc[:, :, D], 0.0, None, ALU.is_equal).then_inc(empty_done, 1)
                dve.wait_ge(empty_done, c + 1)
                dve.scalar_tensor_tensor(total[:], empty[:], y_total[:, D:ACC_W], acc[:, :, D], ALU.mult,
                                         ALU.add).then_inc(total_ready, 1)
                dve.wait_ge(total_ready, c + 1)
                dve.reciprocal(weight[:], total[:]).then_inc(weight_done, 1)
                dve.wait_ge(weight_done, c + 1)
                dve.tensor_scalar(out_weight[:], weight[:], out_scale[:, 0:1], None, ALU.mult).then_inc(out_weight_done, 1)

            def spread(c, j):
                dve.scalar_tensor_tensor(acc[:, cols(j, 1), 0:D].rearrange("p a d -> p (a d)"), y_total[:, 0:D],
                                         empty[:, cols(j, 1)], acc[:, cols(j, 1), 0:D].rearrange("p a d -> p (a d)"),
                                         ALU.mult, ALU.add).then_inc(spread_done, 1)

            def finish(c, j):
                dve.wait_ge(spread_done, CHUNK_TILES * c + (j + 1))
                dve.wait_ge(out_weight_done, c + 1)
                rows = tile_of(x_sb, c * CHUNK_TILES + j)
                dve.scalar_tensor_tensor(rows, acc[:, cols(j, 1), 0:D].rearrange("p a d -> p (a d)"),
                                         out_weight[:, cols(j, 1)], rows, ALU.mult, ALU.add).then_inc(finished, 1)

            def round_(c, r, first_round=False, first_chunk=False, y_prep=False, last_chunk=False, last_round=False):
                k = c * ROUNDS + r
                for u in range(UNROLL):
                    i = c * MT + (r * UNROLL + u)
                    if not (last_round and u == UNROLL - 1):
                        mask(i + 1, u + 1, k + (u + 1) // UNROLL)
                    if u == 1 and not last_chunk:
                        dve.wait_ge(tile_bn, begun(k + X_AHEAD))
                    dve.wait_ge(hi_ready, i + 1)
                    dve.scalar_tensor_tensor(w_lo[:, u, :], e[:, u, :], PSCALE, w_hi[:, u, :], ALU.mult,
                                             ALU.subtract).then_inc(lo_ready, 1)
                    if first_round and u == 1 and not first_chunk:
                        weigh(c - 1)
                    if u == 2 and not first_chunk:
                        spread(c - 1, r)
                    if u == 3 and not first_chunk:
                        finish(c - 1, r)
                    if u == 0 and not last_chunk:
                        tile_stats(k + X_AHEAD)
                    if u == 1 and y_prep:
                        y_lo(r + Y_AHEAD, misc[:])
                    if u == 1 and not last_chunk:
                        tile_mean()
                        tile_add_half(k + X_AHEAD - 1)
                    if u == 2 and not last_chunk:
                        tile_clip(k + X_AHEAD, False)
                    if u == 2 and y_prep:
                        v_lo(r + Y_AHEAD)
                    if u == 3 and not last_chunk:
                        tile_low(k + X_AHEAD - 1)

            def total_of_y():
                dve.wait_ge(total_summed, 1)
                dve.tensor_scalar(y_total[:, 0:D], misc[:, 0:D], y_scale[:, 0:1], None, ALU.mult).then_inc(total_done, 1)

            mask(0, 0, 0)
            dve.wait_ge(half0_done, 1)
            for t in range(CHUNK_TILES):
                last = dve.scalar_tensor_tensor(x_sb[:, t, :], relu0[:, t, :], half_rstd0[:, t:t + 1], x_sb[:, t, :],
                                                ALU.mult, ALU.add)
            last.then_inc(finished, 1)
            tile_low(CHUNK_TILES)
            tile_stats(CHUNK_TILES + 1)
            dve.wait_ge(tile_bn, 2)
            tile_mean()
            tile_clip(CHUNK_TILES + 1, False)
            dve.wait_ge(padded, 3)
            sweep(dve, round_, total_of_y)
            weigh(NC - 1)
            for j in range(CHUNK_TILES):
                spread(NC - 1, j)
            for j in range(CHUNK_TILES):
                finish(NC - 1, j)

        @block.tensor
        def _(pe):
            def score(i, u):
                tile = (i % MT) * P
                first = (i // MT) * CW
                s = scores[u % 2]
                for lhs, parts in ((yt_hi, (xt_hi, xt_lo)), (yt_lo, (xt_hi,))):
                    for part in parts:
                        for h in range(CW // BANK):
                            last = pe.matmul(s[:, h * BANK:(h + 1) * BANK], lhs[:, cols(tile, P)],
                                             part[:, cols(first + h * BANK, BANK)],
                                             start=(lhs is yt_hi and part is xt_hi), stop=(lhs is yt_lo))
                last.then_inc(scores_ready, 1)

            def add_values(t, u, first, last_step):
                high = v[:, cols(t, 1), 0:ACC_W].rearrange("p a w -> p (a w)")
                low = v[:, cols(t, 1), ACC_W:VW].rearrange("p a w -> p (a w)")
                for j in range(CHUNK_TILES):
                    o = (j % PER_BANK) * ACC_W
                    bank = sums[j // PER_BANK]
                    pe.matmul(bank[:, o:o + ACC_W], w_hi[:, u, j * P:(j + 1) * P], high,
                              start=first and j % PER_BANK == 0, stop=False, skip_group_check=True)
                    pe.matmul(bank[:, o:o + D], w_hi[:, u, j * P:(j + 1) * P], low,
                              start=False, stop=False, skip_group_check=True)
                    last = pe.matmul(bank[:, o:o + ACC_W], w_lo[:, u, j * P:(j + 1) * P], high,
                                     start=False, stop=last_step, skip_group_check=True)
                return last

            def turn_batch(src, dst):
                for j in range(UNROLL):
                    last = pe.transpose(dst[:, j * P:(j + 1) * P], src[:, j, :], ident[:])
                last.then_inc(y_turned, 1)

            def turn_tile(n):
                pe.wait_ge(tile_unit, begun(n))
                pe.transpose(misc[:, 0:P], unit_t[:], ident[:]).then_inc(tile_turned, 1)

            pe.wait_ge(consts_ready, 3)
            pe.wait_ge(unit0_done, 1)
            for t in range(CHUNK_TILES):
                last = pe.transpose(scores[0][:, t * P:(t + 1) * P], unit0[:, t, :], ident[:])
            last.then_inc(turned0, 1)
            for b in range(Y_AHEAD):
                pe.wait_ge(y_unit_dve, b + 1)
                turn_batch(y_unit0[:, b * UNROLL:(b + 1) * UNROLL, :], sums[b])
            pe.wait_ge(ymax_step, 1)
            pe.matmul(misc[0:1, 0:P], ymax_p[:], ident[:], start=True, stop=True).then_inc(ymax_moved, 1)
            pe.wait_ge(split0, 1)
            pe.wait_ge(y_split, 1)
            score(0, 0)
            score(1, 1)
            pe.wait_ge(ymax_step, 2)
            pe.matmul(misc[:, P:P + 1], ones[0:1, :], ymax_1[:], start=True, stop=True).then_inc(ymax_moved, 1)
            pe.wait_ge(ymax_done, 1)
            turn_tile(CHUNK_TILES)
            pe.wait_ge(y_split, Y_AHEAD)

            def round_(c, r, first_round=False, first_chunk=False, y_prep=False, last_chunk=False, last_round=False):
                k = c * ROUNDS + r
                for u in range(UNROLL):
                    i = c * MT + (r * UNROLL + u)
                    if u == 0 and y_prep:
                        pe.wait_ge(y_unit_pool, r + 1)
                        pe.wait_ge(tile_split, begun(k + X_AHEAD - 2))
                        turn_batch(y_unit_b, misc)
                    if u == 2 and not last_chunk:
                        if y_prep:
                            pe.wait_ge(y_split, r + Y_AHEAD + 1)
                        pe.wait_ge(tile_split, begun(k + X_AHEAD - 2))
                        turn_tile(k + X_AHEAD - 1)
                    if not (last_round and u >= UNROLL - 2):
                        pe.wait_ge(exp_ready, i + 1)
                        score(i + 2, u)
                    if first_round and u == 0 and first_chunk:
                        continue
                    pe.wait_ge(lo_ready, i)
                    if u == 1 and first_chunk:
                        pe.wait_ge(v_ready, r + 1)
                    if first_round and u == 1 and not first_chunk:
                        pe.wait_ge(acc_copied, c)
                    last = add_values((r * UNROLL + (u - 1)) % MT, (u - 1) % UNROLL, first_round and u == 1,
                                      first_round and u == 0)
                    if u == 0:
                        last.then_inc(round_summed, 1)

            def total_of_y():
                pe.wait_ge(folded, 5)
                pe.wait_ge(tile_split, begun(Y_ROUNDS - 1 + X_AHEAD - 1))
                pe.matmul(misc[:, 0:D], ones[:], fold[:, 0, :], start=True, stop=True).then_inc(total_summed, 1)
                pe.wait_ge(total_done, 1)

            sweep(pe, round_, total_of_y)
            pe.wait_ge(lo_ready, STEPS)
            add_values(MT - 1, UNROLL - 1, False, True).then_inc(round_summed, 1)


def kernel(x, adj, L0_gnn_y):
    import concourse.bacc as bacc
    from concourse.bass_utils import run_bass_kernel_spmd

    x, adj, y = np.asarray(x), np.asarray(adj), np.asarray(L0_gnn_y)
    y_rows = y.reshape(P, MT, D)
    arrays = {
        "x": np.ascontiguousarray(x.reshape(P, NT, D)),
        "y": np.ascontiguousarray(y_rows),
        "adj_t": np.ascontiguousarray(
            adj.reshape(P, NC, CHUNK_TILES, P, MT).transpose(1, 4, 3, 2, 0).reshape(STEPS, P, CW)),
    }
    nc = bacc.Bacc("TRN2", target_bir_lowering=False, num_devices=1)
    aps = {name: nc.dram_tensor(name, a.shape, mybir.dt.from_np(a.dtype), kind="ExternalInput").ap()
           for name, a in arrays.items()}
    out = nc.dram_tensor("out", (P, NT, D), mybir.dt.float32, kind="ExternalOutput").ap()
    build(nc, aps["x"], aps["y"], aps["adj_t"], out)
    result = run_bass_kernel_spmd(nc, [arrays], core_ids=[0])
    return result.results[0]["out"].reshape(N, D)
```

```python
from contextlib import ExitStack

import numpy as np
import concourse.bass as bass
from concourse import mybir

P = 128
N = 4096
M = 4096
D = 128
NT = N // P
MT = M // P
CHUNK_TILES = 8
CW = CHUNK_TILES * P
NC = NT // CHUNK_TILES
STEPS = NC * MT
UNROLL = 4
ROUNDS = MT // UNROLL
BATCHES = MT // UNROLL
BW = UNROLL * P
BANK = 512
ACC_W = D + 1
PER_BANK = BANK // ACC_W
ACC_BANKS = -(-CHUNK_TILES // PER_BANK)
VW = 2 * D + 1
Y_AHEAD = 2
X0 = CHUNK_TILES + 1
X_AHEAD = X0 + 1
STORE_TILES = 4
LN_EPS = 1e-5
NORM_EPS = 1e-8
SCALE = 2.0 ** 14
PSCALE = 2.0 ** 12
Y_FLOOR = (NORM_EPS / SCALE) ** 2
X_FLOOR = (NORM_EPS / SCALE) ** 2 / 4
Y_SUMSQ_ACT = 22
Y_SUMSQ_BREAKS = (10, 12)
WARM_UP = 12
LAST_MASK = CW * 5 // 8
TAIL_POOL = 2
X0_UNIT_DVE = 7
X0_DVE = 5
X0_HALF = CHUNK_TILES // 2


def build(nc, x, y, adj_t, out):
    f32, f16 = mybir.dt.float32, mybir.dt.float16
    ALU, ACT, AX = mybir.AluOpType, mybir.ActivationFunctionType, mybir.AxisListType

    with ExitStack() as ctx:
        def sb(name, shape, dt=f32):
            return ctx.enter_context(nc.sbuf_tensor(name, shape, dt))

        def sem(name):
            return ctx.enter_context(nc.semaphore(name))

        x_sb = sb("x_sb", [P, NT + X_AHEAD - CHUNK_TILES, D])
        y_sb = sb("y_sb", [P, MT, D])
        y_unit0 = sb("y_unit0", [P, UNROLL, D])
        y_unit_b = sb("y_unit_b", [P, UNROLL, D])
        relu0 = sb("relu0", [P, X0, D])
        unit0 = sb("unit0", [P, X0, D])
        relu_t = sb("relu_t", [P, D])
        unit_t = sb("unit_t", [P, D])
        act_junk = sb("act_junk", [P, D])
        xt_hi = sb("xt_hi", [P, N + (X_AHEAD - CHUNK_TILES) * P], f16)
        xt_lo = sb("xt_lo", [P, N + (X_AHEAD - CHUNK_TILES) * P], f16)
        yt_hi = sb("yt_hi", [P, M], f16)
        yt_lo = sb("yt_lo", [P, M], f16)
        v = sb("v", [P, MT, VW], f16)
        adj = sb("adj", [P, UNROLL, CW])
        e = sb("e", [P, UNROLL, CW])
        w_hi = sb("w_hi", [P, UNROLL, CW], f16)
        w_lo = sb("w_lo", [P, UNROLL, CW], f16)
        acc = sb("acc", [P, CHUNK_TILES, ACC_W])
        ident = sb("ident", [P, P])
        ones = sb("ones", [P, P])
        neg_half = sb("neg_half", [P, MT])
        bn0 = sb("bn0", [P, X0, 6])
        moments0 = sb("moments0", [P, X0, 2])
        var4_0 = sb("var4_0", [P, X0])
        neg_mean0 = sb("neg_mean0", [P, X0])
        half_rstd0 = sb("half_rstd0", [P, X0])
        sumsq0 = sb("sumsq0", [P, X0])
        floored0 = sb("floored0", [P, X0])
        unit_scale0 = sb("unit_scale0", [P, X0])
        bn_t = sb("bn_t", [P, 6])
        moments_t = sb("moments_t", [P, 2])
        var4_t = sb("var4_t", [P, 1])
        half_rstd_t = sb("half_rstd_t", [P, 1])
        sumsq_t = sb("sumsq_t", [P, 1])
        floored_t = sb("floored_t", [P, 1])
        unit_scale_t = sb("unit_scale_t", [P, 1])
        y_sumsq = sb("y_sumsq", [P, MT])
        y_floored = sb("y_floored", [P, MT])
        y_unit_scale = sb("y_unit_scale", [P, MT])
        ymax_p = sb("ymax_p", [P, 1])
        ymax_1 = sb("ymax_1", [1, 1])
        ymax = sb("ymax", [P, 1])
        y_scale = sb("y_scale", [P, 1])
        y_rscale = sb("y_rscale", [P, 1])
        out_scale = sb("out_scale", [P, 1])
        fold = sb("fold", [P, UNROLL, D])
        squares = sb("squares", [P, MT - Y_SUMSQ_ACT, D])
        v_full = sb("v_full", [P, UNROLL, D])
        half_h = sb("half_h", [P, D])
        tail_a = sb("tail_a", [P, TAIL_POOL, D])
        tail_b = sb("tail_b", [P, TAIL_POOL, D])
        y_total = sb("y_total", [P, ACC_W])
        empty = sb("empty", [P, CHUNK_TILES])
        total = sb("total", [P, CHUNK_TILES])
        weight = sb("weight", [P, CHUNK_TILES])
        out_weight = sb("out_weight", [P, CHUNK_TILES])

        scores = [ctx.enter_context(nc.psum_tensor(f"scores{i}", [P, CW], f32)) for i in range(2)]
        sums = [ctx.enter_context(nc.psum_tensor(f"sums{i}", [P, BANK], f32)) for i in range(ACC_BANKS)]
        misc = ctx.enter_context(nc.psum_tensor("misc", [P, BANK], f32))

        x_landed, x_rest_landed = sem("x_landed"), sem("x_rest_landed")
        y_landed = [sem(f"y_landed{b}") for b in range(4)]
        adj_landed = [sem(f"adj_landed{u}") for u in range(UNROLL)]
        zeroed, consts_ready, padded = sem("zeroed"), sem("consts_ready"), sem("padded")
        bn0_done, moments0_done, var0_done, half0_done = (sem("bn0_done"), sem("moments0_done"), sem("var0_done"),
                                                          sem("half0_done"))
        relu0_dve, relu0_act, sumsq0_dve, sumsq0_act = (sem("relu0_dve"), sem("relu0_act"), sem("sumsq0_dve"),
                                                        sem("sumsq0_act"))
        floored0_done, scale0_done, unit0_dve, unit0_act = (sem("floored0_done"), sem("scale0_done"),
                                                            sem("unit0_dve"), sem("unit0_act"))
        turned0, hi0_done, split0, half_h0 = sem("turned0"), sem("hi0_done"), sem("split0"), sem("half_h0")
        tile_bn, tile_moments, tile_relu, tile_var = (sem("tile_bn"), sem("tile_moments"), sem("tile_relu"),
                                                      sem("tile_var"))
        tile_half, tile_residual, tile_sumsq, tile_floored = (sem("tile_half"), sem("tile_residual"),
                                                              sem("tile_sumsq"), sem("tile_floored"))
        tile_half_h = sem("tile_half_h")
        tile_scale, tile_unit, tile_turned, tile_hi, tile_split = (sem("tile_scale"), sem("tile_unit"),
                                                                   sem("tile_turned"), sem("tile_hi"),
                                                                   sem("tile_split"))
        y_sumsq_act, y_sumsq_dve, y_floor_done, y_scales_done = (sem("y_sumsq_act"), sem("y_sumsq_dve"),
                                                                 sem("y_floor_done"), sem("y_scales_done"))
        ymax_step, ymax_moved, ymax_done, y_scale_done = (sem("ymax_step"), sem("ymax_moved"), sem("ymax_done"),
                                                          sem("y_scale_done"))
        y_rscale_done, folded, total_summed, total_done = (sem("y_rscale_done"), sem("folded"), sem("total_summed"),
                                                           sem("total_done"))
        y_unit_dve, y_unit_pool, y_turned, y_hi_done, y_split = (sem("y_unit_dve"), sem("y_unit_pool"),
                                                                 sem("y_turned"), sem("y_hi_done"), sem("y_split"))
        v_hi_done, v_full_done, v_ready = sem("v_hi_done"), sem("v_full_done"), sem("v_ready")
        rest_masked = sem("rest_masked")
        scores_ready, exp_ready, masked = sem("scores_ready"), sem("exp_ready"), sem("masked")
        hi_ready, lo_ready = sem("hi_ready"), sem("lo_ready")
        round_summed, acc_copied = sem("round_summed"), sem("acc_copied")
        empty_done, total_ready, weight_done, out_weight_done = (sem("empty_done"), sem("total_ready"),
                                                                 sem("weight_done"), sem("out_weight_done"))
        tail_step, tail_stored = sem("tail_step"), sem("tail_stored")
        spread_done, finished, out_stored = sem("spread_done"), sem("finished"), sem("out_stored")

        block = ctx.enter_context(nc.Block())

        def cols(start, size):
            return bass.ds(start, size)

        def tile_of(tensor, t):
            return tensor[:, cols(t, 1), :].rearrange("p a d -> p (a d)")

        def batch_of(tensor, b):
            return tensor[:, cols(b * UNROLL, UNROLL), :]

        FOLDS = UNROLL.bit_length() - 1
        Y_ROUNDS = BATCHES - Y_AHEAD

        def sweep(eng, round_, after_chunk0=None):
            round_(0, 0, first_round=True, first_chunk=True, y_prep=True)
            with eng.Fori(1, Y_ROUNDS) as r:
                round_(0, r, first_chunk=True, y_prep=True)
            with eng.Fori(Y_ROUNDS, ROUNDS) as r:
                round_(0, r, first_chunk=True)
            if after_chunk0:
                after_chunk0()
            with eng.Fori(1, NC - 1) as c:
                round_(c, 0, first_round=True)
                with eng.Fori(1, ROUNDS) as r:
                    round_(c, r)
            round_(NC - 1, 0, first_round=True, last_chunk=True)
            with eng.Fori(1, ROUNDS - 1) as r:
                round_(NC - 1, r, last_chunk=True)
            round_(NC - 1, ROUNDS - 1, last_chunk=True, last_round=True)

        def begun(n):
            return n - (X0 - 1)

        @block.sync
        def _(sp):
            sp.dma_start(x_sb[:, 0:X_AHEAD, :], x[:, 0:X_AHEAD, :]).then_inc(x_landed, 16)
            for q in range(4):
                w = MT // 4
                sp.dma_start(y_sb[:, q * w:(q + 1) * w, :], y[:, q * w:(q + 1) * w, :]).then_inc(y_landed[q], 16)
            sp.dma_start(adj[:, 0, :], adj_t[0]).then_inc(adj_landed[0], 16)
            sp.dma_start(x_sb[:, X_AHEAD:NT, :], x[:, X_AHEAD:NT, :]).then_inc(x_rest_landed, 16)
            for u in range(1, UNROLL):
                sp.dma_start(adj[:, u, :], adj_t[u]).then_inc(adj_landed[u], 16)
            with sp.Fori(1, STEPS // UNROLL) as r:
                for u in range(UNROLL):
                    sp.wait_ge(masked, UNROLL * r + (u - UNROLL + 1))
                    sp.dma_start(adj[:, u, :], adj_t[cols(UNROLL * r + u, 1)].rearrange("a p w -> (a p) w")
                                 ).then_inc(adj_landed[u], 16)
            for j in range(0, CHUNK_TILES, STORE_TILES):
                first = (NC - 1) * CHUNK_TILES + j
                sp.wait_ge(finished, min(first + STORE_TILES, NT - TAIL_POOL) + 1)
                if j + STORE_TILES == CHUNK_TILES:
                    sp.wait_ge(tail_step, 4)
                sp.dma_start(out[:, first:first + STORE_TILES, :], x_sb[:, first:first + STORE_TILES, :]
                             ).then_inc(tail_stored, 16)
            sp.wait_ge(out_stored, 16 * (NC - 1))
            sp.wait_ge(tail_stored, 16 * (CHUNK_TILES // STORE_TILES))

        @block.gpsimd
        def _(pool):
            pool.memset(neg_half[:], -0.5).then_inc(consts_ready, 1)
            pool.memset(ident[:], 0.0).then_inc(zeroed, 1)
            pool.memset(ones[:], 1.0).then_inc(consts_ready, 1)
            pool.wait_ge(zeroed, 1)
            pool.affine_select(out=ident[:], in_=ident[:], compare_op=ALU.not_equal, fill=1.0, base=0,
                               pattern=[[-1, P]], channel_multiplier=1).then_inc(consts_ready, 1)
            pool.memset(v[:, :, D:D + 1], 1.0).then_inc(padded, 1)
            pool.memset(y_total[:, D:ACC_W], float(M)).then_inc(padded, 1)
            pool.memset(x_sb[:, NT:, :], 0.0).then_inc(padded, 1)
            pool.memset(fold[:], 0.0).then_inc(folded, 1)
            pool.wait_ge(consts_ready, 3)

            def y_floor(t0, t1, done):
                pool.tensor_scalar(y_floored[:, t0:t1], y_sumsq[:, t0:t1], Y_FLOOR, None,
                                   ALU.max).then_inc(y_floor_done, 1)
                pool.wait_ge(y_floor_done, done)

            def y_scales(t0, t1):
                pool.tensor_tensor(y_unit_scale[:, t0:t1], y_floored[:, t0:t1], neg_half[:, t0:t1],
                                   ALU.pow).then_inc(y_scales_done, 1)

            def y_scales_of(b):
                pool.tensor_tensor(y_unit_scale[:, cols(b * UNROLL, UNROLL)], y_floored[:, cols(b * UNROLL, UNROLL)],
                                   neg_half[:, 0:UNROLL], ALU.pow).then_inc(y_scales_done, 1)

            def batch_to_unit(b):
                pool.wait_ge(y_scales_done, b + 1)
                pool.wait_ge(y_turned, b)
                tiles = cols(b * UNROLL, UNROLL)
                pool.tensor_tensor(y_unit_b[:], y_sb[:, tiles, :],
                                   y_unit_scale[:, tiles].unsqueeze(2).to_broadcast([P, UNROLL, D]),
                                   ALU.mult).then_inc(y_unit_pool, 1)

            pool.wait_ge(y_sumsq_act, UNROLL)
            y_floor(0, UNROLL, 1)
            y_scales(0, UNROLL)
            for part, (t0, t1) in enumerate(((0, X0_HALF), (X0_HALF, X0))):
                pool.wait_ge(floored0_done, part + 1)
                pool.tensor_tensor(unit_scale0[:, t0:t1], floored0[:, t0:t1], neg_half[:, t0:t1],
                                   ALU.pow).then_inc(scale0_done, 1)
            first = Y_AHEAD * UNROLL
            pool.wait_ge(y_sumsq_act, first)
            y_floor(UNROLL, first, 2)
            y_scales(UNROLL, first)
            batch_to_unit(1)
            pool.wait_ge(y_sumsq_act, Y_SUMSQ_ACT)
            pool.wait_ge(y_sumsq_dve, MT - Y_SUMSQ_ACT)
            y_floor(first, MT, 3)
            y_scales(first, first + UNROLL)
            pool.wait_ge(ymax_done, 1)
            pool.tensor_tensor(y_scale[:], ymax[:], neg_half[:, 0:1], ALU.pow).then_inc(y_scale_done, 1)

            def tile_scales(n, first=False):
                pool.wait_ge(tile_var, begun(n))
                if not first:
                    pool.wait_ge(tile_residual, begun(n - 1))
                    pool.wait_ge(tile_unit, begun(n - 1))
                pool.wait_ge(tile_sumsq, begun(n))
                pool.tensor_tensor(half_rstd_t[:], var4_t[:], neg_half[:, 0:1], ALU.pow).then_inc(tile_half, 1)
                pool.tensor_scalar(floored_t[:], var4_t[:], X_FLOOR, sumsq_t[:, 0:1], ALU.mult,
                                   ALU.max).then_inc(tile_floored, 1)
                pool.wait_ge(tile_floored, begun(n))
                pool.tensor_tensor(unit_scale_t[:], floored_t[:], neg_half[:, 0:1], ALU.pow).then_inc(tile_scale, 1)
                pool.wait_ge(tile_half, begun(n))
                pool.tensor_tensor(half_h[:], relu_t[:], half_rstd_t[:].to_broadcast([P, D]),
                                   ALU.mult).then_inc(tile_half_h, 1)
                pool.wait_ge(tile_half_h, begun(n))
                pool.tensor_tensor(tile_of(x_sb, n), tile_of(x_sb, n), half_h[:], ALU.add).then_inc(tile_residual, 1)

            def v_low(b):
                pool.wait_ge(v_ready, b)
                pool.tensor_tensor(v_full[:], batch_of(y_sb, b), y_scale[:].unsqueeze(2).to_broadcast([P, UNROLL, D]),
                                   ALU.mult).then_inc(v_full_done, 1)
                pool.wait_ge(v_full_done, b)
                pool.wait_ge(v_hi_done, b + 1)
                pool.tensor_tensor(v[:, cols(b * UNROLL, UNROLL), D + 1:VW], v_full[:],
                                   v[:, cols(b * UNROLL, UNROLL), 0:D], ALU.subtract).then_inc(v_ready, 1)

            def add_batch(b):
                pool.wait_ge(folded, b + 1)
                pool.tensor_tensor(fold[:], fold[:], batch_of(y_sb, b), ALU.add).then_inc(folded, 1)

            batch_to_unit(Y_AHEAD)
            tile_scales(X0, True)
            v_low(1)
            with pool.Fori(0, Y_ROUNDS - 1) as r:
                b = r + Y_AHEAD + 1
                y_scales_of(b)
                batch_to_unit(b)
                v_low(r + Y_AHEAD)
                add_batch(r)
                tile_scales(r + X_AHEAD)
            v_low(BATCHES - 1)
            folds = BATCHES
            for b in range(Y_ROUNDS - 1, ROUNDS):
                add_batch(b)
            half = UNROLL
            while half > 1:
                half //= 2
                folds += 1
                pool.wait_ge(folded, folds)
                pool.tensor_tensor(fold[:, 0:half, :], fold[:, 0:half, :], fold[:, half:2 * half, :],
                                   ALU.add).then_inc(folded, 1)
            pool.tensor_tensor(half_rstd0[:], var4_0[:], neg_half[:, 0:X0], ALU.pow).then_inc(half0_done, 1)
            tile_scales(Y_ROUNDS - 1 + X_AHEAD)
            pool.wait_ge(half0_done, 1)
            pool.tensor_tensor(relu0[:], relu0[:], half_rstd0[:].unsqueeze(2).to_broadcast([P, X0, D]),
                               ALU.mult).then_inc(half_h0, 1)
            pool.wait_ge(half_h0, 1)
            pool.tensor_tensor(x_sb[:, 0:X0, :], x_sb[:, 0:X0, :], relu0[:],
                               ALU.add).then_inc(finished, 1)

            def store(c):
                pool.wait_ge(finished, CHUNK_TILES * (c + 1) + 1)
                pool.dma_start(out[:, cols(c * CHUNK_TILES, CHUNK_TILES), :],
                               x_sb[:, cols(c * CHUNK_TILES, CHUNK_TILES), :]).then_inc(out_stored, 16)

            with pool.Fori(Y_ROUNDS, ROUNDS) as r:
                tile_scales(r + X_AHEAD)
            with pool.Fori(1, NC - 1) as c:
                with pool.Fori(0, ROUNDS) as r:
                    tile_scales(c * ROUNDS + r + X_AHEAD)
                store(c - 1)
            pool.wait_ge(exp_ready, STEPS)
            pool.wait_ge(adj_landed[UNROLL - 1], 16 * (STEPS // UNROLL))
            pool.tensor_tensor(e[:, UNROLL - 1, LAST_MASK:], adj[:, UNROLL - 1, LAST_MASK:],
                               e[:, UNROLL - 1, LAST_MASK:], ALU.mult).then_inc(rest_masked, 1)
            store(NC - 2)
            t0 = CHUNK_TILES - TAIL_POOL
            shape = [P, TAIL_POOL, D]
            pool.wait_ge(acc_copied, ACC_BANKS * NC)
            pool.wait_ge(empty_done, NC)
            pool.tensor_tensor(tail_a[:], y_total[:, 0:D].unsqueeze(1).to_broadcast(shape),
                               empty[:, t0:].unsqueeze(2).to_broadcast(shape), ALU.mult).then_inc(tail_step, 1)
            pool.wait_ge(tail_step, 1)
            pool.tensor_tensor(tail_b[:], tail_a[:], acc[:, t0:, 0:D], ALU.add).then_inc(tail_step, 1)
            pool.wait_ge(tail_step, 2)
            pool.wait_ge(out_weight_done, NC)
            pool.tensor_tensor(tail_a[:], tail_b[:], out_weight[:, t0:].unsqueeze(2).to_broadcast(shape),
                               ALU.mult).then_inc(tail_step, 1)
            pool.wait_ge(tail_step, 3)
            pool.tensor_tensor(x_sb[:, NT - TAIL_POOL:NT, :], x_sb[:, NT - TAIL_POOL:NT, :], tail_a[:],
                               ALU.add).then_inc(tail_step, 1)

        @block.scalar
        def _(act):
            def y_squares(t0, t1):
                for t in range(t0, t1):
                    if t == t0 or t % (MT // 4) == 0:
                        act.wait_ge(y_landed[t // (MT // 4)], 16)
                    slot, place = t // CHUNK_TILES, t % CHUNK_TILES * D
                    act.activation(e[:, slot, place:place + D], y_sb[:, t, :], ACT.Square, scale=1.0 / SCALE,
                                   accum_out=y_sumsq[:, t:t + 1]).then_inc(y_sumsq_act, 1)

            def y_hi(b, src):
                act.wait_ge(y_turned, b + 1)
                act.copy(yt_hi[:, cols(b * BW, BW)], src).then_inc(y_hi_done, 1)

            def v_hi(b):
                act.activation(v[:, cols(b * UNROLL, UNROLL), 0:D], batch_of(y_sb, b), ACT.Copy,
                               scale=y_scale[:, 0:1]).then_inc(v_hi_done, 1)

            def tile_squares(n):
                act.wait_ge(tile_relu, begun(n))
                act.activation(act_junk[:], relu_t[:], ACT.Square, scale=1.0 / SCALE,
                               accum_out=sumsq_t[:]).then_inc(tile_sumsq, 1)

            def tile_to_unit(n, first):
                act.wait_ge(tile_scale, begun(n))
                if not first:
                    act.wait_ge(tile_turned, begun(n - 1))
                act.activation(unit_t[:], relu_t[:], ACT.Copy, scale=unit_scale_t[:, 0:1]).then_inc(tile_unit, 1)

            def tile_high(n):
                act.wait_ge(tile_turned, begun(n))
                act.copy(xt_hi[:, cols(n * P, P)], misc[:, 0:P]).then_inc(tile_hi, 1)

            y_squares(0, UNROLL)
            act.wait_ge(var0_done, 2)
            for t in range(X0_DVE, X0):
                act.activation(relu0[:, t, :], x_sb[:, t, :], ACT.Relu,
                               bias=neg_mean0[:, t:t + 1]).then_inc(relu0_act, 1)
            for t in range(X0_DVE, X0):
                act.wait_ge(relu0_act, t - X0_DVE + 1)
                act.activation(unit0[:, t, :], relu0[:, t, :], ACT.Square, scale=1.0 / SCALE,
                               accum_out=sumsq0[:, t:t + 1]).then_inc(sumsq0_act, 1)
            y_squares(UNROLL, Y_SUMSQ_BREAKS[0])
            y_hi(0, sums[0][:])
            act.wait_ge(sumsq0_act, X0 - X0_DVE)
            act.wait_ge(scale0_done, 2)
            for t in range(X0_UNIT_DVE, X0):
                act.activation(unit0[:, t, :], relu0[:, t, :], ACT.Copy,
                               scale=unit_scale0[:, t:t + 1]).then_inc(unit0_act, 1)
            act.wait_ge(turned0, 1)
            act.copy(xt_hi[:, 0:BANK], scores[0][:, 0:BANK]).then_inc(hi0_done, 1)
            y_squares(Y_SUMSQ_BREAKS[0], Y_SUMSQ_BREAKS[1])
            act.wait_ge(turned0, 2)
            act.copy(xt_hi[:, BANK:CW], scores[0][:, BANK:CW]).then_inc(hi0_done, 1)
            act.copy(xt_hi[:, CW:CW + P], sums[2][:, 0:P]).then_inc(hi0_done, 1)
            y_squares(Y_SUMSQ_BREAKS[1], Y_SUMSQ_ACT)

            def exp_scores(i, u):
                act.wait_ge(scores_ready, i + 1)
                act.activation(e[:, u % UNROLL, :], scores[u % 2][:], ACT.Exp,
                               scale=1.0 / SCALE ** 2).then_inc(exp_ready, 1)

            def evacuate(c, last=False):
                act.wait_ge(finished, CHUNK_TILES * c + 1)
                act.wait_ge(round_summed, ROUNDS * (c + 1))
                for b in range(ACC_BANKS):
                    if last:
                        act.wait_ge(round_summed, ROUNDS * (c + 1) + b)
                    j0, j1 = b * PER_BANK, min((b + 1) * PER_BANK, CHUNK_TILES)
                    act.copy(acc[:, j0:j1, :], sums[b][:, 0:(j1 - j0) * ACC_W]).then_inc(acc_copied, 1)

            def round_(c, r, first_round=False, first_chunk=False, y_prep=False, last_chunk=False, last_round=False):
                k = c * ROUNDS + r
                for u in range(UNROLL):
                    i = c * MT + (r * UNROLL + u)
                    very_first = first_round and first_chunk and u == 0
                    if not (last_round and u == UNROLL - 1) and not very_first:
                        exp_scores(i + 1, u + 1)
                    if first_round and u == 1 and not first_chunk:
                        evacuate(c - 1)
                    act.wait_ge(masked, i + 1)
                    if last_round and u == UNROLL - 1:
                        act.wait_ge(rest_masked, 1)
                    act.activation(w_hi[:, u, :], e[:, u, :], ACT.Copy, scale=PSCALE).then_inc(hi_ready, 1)
                    if very_first:
                        exp_scores(1, 1)
                        act.wait_ge(y_scale_done, 1)
                        act.wait_ge(padded, 1)
                        v_hi(0)
                        tile_squares(X0)
                        v_hi(1)
                        y_hi(Y_AHEAD, misc[:])
                    if u == (1 if first_round else 0) and y_prep:
                        v_hi(r + Y_AHEAD)
                    if u == 1 and y_prep and not first_round:
                        y_hi(r + Y_AHEAD, misc[:])
                    if u == 1 and not last_chunk:
                        tile_to_unit(k + X_AHEAD - 1, first_round and first_chunk)
                    if u == 3 and not last_chunk:
                        tile_high(k + X_AHEAD - 1)
                        tile_squares(k + X_AHEAD)

            act.wait_ge(y_sumsq_act, Y_SUMSQ_ACT)
            exp_scores(0, 0)
            y_hi(1, misc[:])
            sweep(act, round_)
            evacuate(NC - 1, last=True)

        @block.vector
        def _(dve):
            def y_squares(t0, t1):
                for t in range(t0, t1):
                    if t == t0 or t % (MT // 4) == 0:
                        dve.wait_ge(y_landed[t // (MT // 4)], 16)
                    dve.tensor_tensor_reduce(squares[:, t - Y_SUMSQ_ACT, :], y_sb[:, t, :], y_sb[:, t, :],
                                             SCALE ** -2, 0.0, ALU.mult, ALU.add,
                                             y_sumsq[:, t:t + 1]).then_inc(y_sumsq_dve, 1)

            def y_lo(b, src):
                dve.wait_ge(y_hi_done, b + 1)
                dve.tensor_tensor(yt_lo[:, cols(b * BW, BW)], src, yt_hi[:, cols(b * BW, BW)],
                                  ALU.subtract).then_inc(y_split, 1)

            def v_lo(b):
                dve.wait_ge(v_hi_done, b + 1)
                dve.scalar_tensor_tensor(v[:, cols(b * UNROLL, UNROLL), D + 1:VW], batch_of(y_sb, b), y_scale[:, 0:1],
                                         v[:, cols(b * UNROLL, UNROLL), 0:D], ALU.mult,
                                         ALU.subtract).then_inc(v_ready, 1)

            def tile_stats(n):
                dve.bn_stats(bn_t[:], tile_of(x_sb, n)).then_inc(tile_bn, 1)

            def tile_mean():
                dve.bn_aggr(moments_t[:], bn_t[:]).then_inc(tile_moments, 1)

            def tile_clip(n, first):
                dve.wait_ge(tile_moments, begun(n))
                if not first:
                    dve.wait_ge(tile_floored, begun(n - 1))
                dve.tensor_scalar(var4_t[:], moments_t[:, 1:2], LN_EPS, 4.0, ALU.add, ALU.mult).then_inc(tile_var, 1)
                if not first:
                    dve.wait_ge(tile_residual, begun(n - 1))
                    dve.wait_ge(tile_unit, begun(n - 1))
                dve.tensor_scalar(relu_t[:], tile_of(x_sb, n), moments_t[:, 0:1], 0.0, ALU.subtract,
                                  ALU.max).then_inc(tile_relu, 1)

            def tile_low(n):
                dve.wait_ge(tile_hi, begun(n))
                dve.tensor_tensor(xt_lo[:, cols(n * P, P)], misc[:, 0:P], xt_hi[:, cols(n * P, P)],
                                  ALU.subtract).then_inc(tile_split, 1)

            dve.wait_ge(x_landed, 16)
            for t in range(X0):
                dve.bn_stats(bn0[:, t, :], x_sb[:, t, :]).then_inc(bn0_done, 1)
            dve.wait_ge(bn0_done, X0)
            for t in range(X0):
                last = dve.bn_aggr(moments0[:, t, :], bn0[:, t, :])
            last.then_inc(moments0_done, 1)
            dve.wait_ge(moments0_done, 1)
            dve.tensor_scalar(neg_mean0[:], moments0[:, :, 0], -1.0, None, ALU.mult).then_inc(var0_done, 1)
            dve.tensor_scalar(var4_0[:], moments0[:, :, 1], LN_EPS, 4.0, ALU.add, ALU.mult).then_inc(var0_done, 1)
            for t in range(X0_DVE):
                dve.tensor_scalar(relu0[:, t, :], x_sb[:, t, :], moments0[:, t, 0:1], 0.0,
                                  ALU.subtract, ALU.max).then_inc(relu0_dve, 1)
            dve.wait_ge(relu0_dve, X0_DVE)
            for t in range(X0_DVE):
                dve.tensor_tensor_reduce(unit0[:, t, :], relu0[:, t, :], relu0[:, t, :], SCALE ** -2, 0.0,
                                         ALU.mult, ALU.add, sumsq0[:, t:t + 1]).then_inc(sumsq0_dve, 1)
            dve.wait_ge(var0_done, 2)
            dve.wait_ge(sumsq0_dve, X0_HALF)
            dve.scalar_tensor_tensor(floored0[:, 0:X0_HALF], var4_0[:, 0:X0_HALF], X_FLOOR, sumsq0[:, 0:X0_HALF],
                                     ALU.mult, ALU.max).then_inc(floored0_done, 1)
            dve.wait_ge(y_scales_done, 1)
            for t in range(UNROLL):
                last = dve.tensor_scalar(y_unit0[:, t, :], y_sb[:, t, :], y_unit_scale[:, t:t + 1], None, ALU.mult)
            last.then_inc(y_unit_dve, 1)
            dve.wait_ge(sumsq0_dve, X0_DVE)
            dve.wait_ge(sumsq0_act, X0 - X0_DVE)
            dve.scalar_tensor_tensor(floored0[:, X0_HALF:X0], var4_0[:, X0_HALF:X0], X_FLOOR, sumsq0[:, X0_HALF:X0],
                                     ALU.mult, ALU.max).then_inc(floored0_done, 1)
            dve.wait_ge(scale0_done, 1)
            for t in range(X0_HALF):
                dve.tensor_scalar(unit0[:, t, :], relu0[:, t, :], unit_scale0[:, t:t + 1], None,
                                  ALU.mult).then_inc(unit0_dve, 1)
            dve.wait_ge(scale0_done, 2)
            for t in range(X0_HALF, X0_UNIT_DVE):
                dve.tensor_scalar(unit0[:, t, :], relu0[:, t, :], unit_scale0[:, t:t + 1], None,
                                  ALU.mult).then_inc(unit0_dve, 1)
            y_lo(0, sums[0][:])
            dve.wait_ge(hi0_done, 1)
            dve.tensor_tensor(xt_lo[:, 0:BANK], scores[0][:, 0:BANK], xt_hi[:, 0:BANK],
                              ALU.subtract).then_inc(split0, 1)
            dve.wait_ge(hi0_done, 2)
            dve.tensor_tensor(xt_lo[:, BANK:CW], scores[0][:, BANK:CW], xt_hi[:, BANK:CW],
                              ALU.subtract).then_inc(split0, 1)
            dve.wait_ge(hi0_done, 3)
            dve.tensor_tensor(xt_lo[:, CW:CW + P], sums[2][:, 0:P], xt_hi[:, CW:CW + P],
                              ALU.subtract).then_inc(split0, 1)
            y_squares(Y_SUMSQ_ACT, MT)
            dve.wait_ge(y_sumsq_act, Y_SUMSQ_ACT)
            dve.wait_ge(y_sumsq_dve, MT - Y_SUMSQ_ACT)
            dve.tensor_reduce(ymax_p[:], y_sumsq[:], AX.X, ALU.max).then_inc(ymax_step, 1)
            tile_stats(X0)
            dve.wait_ge(ymax_moved, 1)
            dve.tensor_reduce(ymax_1[:], sums[1][0:1, 0:P], AX.X, ALU.max).then_inc(ymax_step, 1)

            def mask(i, u, k, w=CW):
                dve.wait_ge(exp_ready, i + 1)
                dve.wait_ge(adj_landed[u % UNROLL], 16 * (k + 1))
                dve.tensor_tensor(e[:, u % UNROLL, 0:w], adj[:, u % UNROLL, 0:w], e[:, u % UNROLL, 0:w],
                                  ALU.mult).then_inc(masked, 1)

            def weigh(c):
                dve.wait_ge(acc_copied, ACC_BANKS * (c + 1))
                dve.wait_ge(finished, 1)
                dve.tensor_scalar(empty[:], acc[:, :, D], 0.0, None, ALU.is_equal).then_inc(empty_done, 1)
                dve.wait_ge(empty_done, c + 1)
                dve.scalar_tensor_tensor(total[:], empty[:], y_total[:, D:ACC_W], acc[:, :, D], ALU.mult,
                                         ALU.add).then_inc(total_ready, 1)

            def weigh_rest(c):
                dve.wait_ge(total_ready, c + 1)
                dve.reciprocal(weight[:], total[:]).then_inc(weight_done, 1)
                dve.wait_ge(weight_done, c + 1)
                dve.tensor_scalar(out_weight[:], weight[:], out_scale[:, 0:1], None,
                                  ALU.mult).then_inc(out_weight_done, 1)

            def spread(c, j):
                dve.scalar_tensor_tensor(acc[:, cols(j, 1), 0:D].rearrange("p a d -> p (a d)"), y_total[:, 0:D],
                                         empty[:, cols(j, 1)], acc[:, cols(j, 1), 0:D].rearrange("p a d -> p (a d)"),
                                         ALU.mult, ALU.add).then_inc(spread_done, 1)

            def finish(c, j):
                dve.wait_ge(spread_done, CHUNK_TILES * c + (j + 1))
                dve.wait_ge(out_weight_done, c + 1)
                rows = tile_of(x_sb, c * CHUNK_TILES + j)
                dve.scalar_tensor_tensor(rows, acc[:, cols(j, 1), 0:D].rearrange("p a d -> p (a d)"),
                                         out_weight[:, cols(j, 1)], rows, ALU.mult, ALU.add).then_inc(finished, 1)

            def round_(c, r, first_round=False, first_chunk=False, y_prep=False, last_chunk=False, last_round=False):
                k = c * ROUNDS + r
                for u in range(UNROLL):
                    i = c * MT + (r * UNROLL + u)
                    very_first = first_round and first_chunk and u == 0
                    if not (last_round and u == UNROLL - 1) and not very_first:
                        mask(i + 1, u + 1, k + (u + 1) // UNROLL, LAST_MASK if last_round and u == UNROLL - 2 else CW)
                    if u == 1 and not last_chunk:
                        dve.wait_ge(tile_bn, begun(k + X_AHEAD))
                    dve.wait_ge(hi_ready, i + 1)
                    dve.scalar_tensor_tensor(w_lo[:, u, :], e[:, u, :], PSCALE, w_hi[:, u, :], ALU.mult,
                                             ALU.subtract).then_inc(lo_ready, 1)
                    if very_first:
                        v_lo(0)
                        mask(1, 1, 0)
                        y_lo(Y_AHEAD, misc[:])
                    if first_round and u == 1 and not first_chunk:
                        weigh(c - 1)
                    if first_round and u == 2 and not first_chunk:
                        weigh_rest(c - 1)
                    if u == (0 if last_round else 2) and not first_chunk:
                        spread(c - 1, r)
                    if u == (1 if last_round else 3) and not first_chunk:
                        finish(c - 1, r)
                    if u == 0 and not last_chunk:
                        tile_stats(k + X_AHEAD)
                    if u == 1 and y_prep and not first_round:
                        y_lo(r + Y_AHEAD, misc[:])
                    if u == 1 and not last_chunk:
                        tile_mean()
                    if u == 2 and not last_chunk:
                        tile_clip(k + X_AHEAD, False)
                    if u == 3 and not last_chunk:
                        tile_low(k + X_AHEAD - 1)

            def total_of_y():
                dve.wait_ge(total_summed, 1)
                dve.tensor_scalar(y_total[:, 0:D], misc[:, 0:D], y_scale[:, 0:1], None,
                                  ALU.mult).then_inc(total_done, 1)

            mask(0, 0, 0)
            dve.wait_ge(ymax_moved, 2)
            dve.tensor_scalar(ymax[:], sums[1][:, P:P + 1], Y_FLOOR, None, ALU.max).then_inc(ymax_done, 1)
            y_lo(1, misc[:])
            dve.wait_ge(tile_bn, 1)
            tile_mean()
            tile_clip(X0, True)
            dve.wait_ge(y_scale_done, 1)
            dve.reciprocal(y_rscale[:], y_scale[:]).then_inc(y_rscale_done, 1)
            dve.wait_ge(y_rscale_done, 1)
            dve.tensor_scalar(out_scale[:], y_rscale[:], 0.5, None, ALU.mult)
            dve.wait_ge(padded, 3)
            dve.wait_ge(x_rest_landed, 16)
            sweep(dve, round_, total_of_y)
            weigh(NC - 1)
            weigh_rest(NC - 1)
            for j0 in range(0, CHUNK_TILES - TAIL_POOL, STORE_TILES):
                tiles = range(j0, min(j0 + STORE_TILES, CHUNK_TILES - TAIL_POOL))
                for j in tiles:
                    spread(NC - 1, j)
                for j in tiles:
                    finish(NC - 1, j)

        @block.tensor
        def _(pe):
            PRODUCTS = ((yt_hi, xt_hi), (yt_hi, xt_lo), (yt_lo, xt_hi))

            def half_score(s, tile, first, lhs, part, h):
                return pe.matmul(s[:, h * BANK:(h + 1) * BANK], lhs[:, cols(tile, P)],
                                 part[:, cols(first + h * BANK, BANK)],
                                 start=(lhs is yt_hi and part is xt_hi), stop=(lhs is yt_lo))

            def score(i, u):
                tile = (i % MT) * P
                first = (i // MT) * CW
                s = scores[u % 2]
                for lhs, part in PRODUCTS:
                    for h in range(CW // BANK):
                        last = half_score(s, tile, first, lhs, part, h)
                last.then_inc(scores_ready, 1)

            def add_values(t, u, first, last_step, c=None, very_last=False):
                high = v[:, cols(t, 1), 0:ACC_W].rearrange("p a w -> p (a w)")
                low = v[:, cols(t, 1), ACC_W:VW].rearrange("p a w -> p (a w)")
                for j in range(CHUNK_TILES):
                    o = (j % PER_BANK) * ACC_W
                    bank = sums[j // PER_BANK]
                    if first and c is not None and j % PER_BANK == 0:
                        pe.wait_ge(acc_copied, ACC_BANKS * (c - 1) + (j // PER_BANK + 1))
                    pe.matmul(bank[:, o:o + ACC_W], w_hi[:, u, j * P:(j + 1) * P], high,
                              start=first and j % PER_BANK == 0, stop=False, skip_group_check=True)
                    pe.matmul(bank[:, o:o + D], w_hi[:, u, j * P:(j + 1) * P], low,
                              start=False, stop=False, skip_group_check=True)
                    last = pe.matmul(bank[:, o:o + ACC_W], w_lo[:, u, j * P:(j + 1) * P], high,
                                     start=False, stop=last_step, skip_group_check=True)
                    if very_last and (j % PER_BANK == PER_BANK - 1 or j == CHUNK_TILES - 1):
                        last.then_inc(round_summed, 1)
                return last

            def turn_batch(src, dst):
                for j in range(UNROLL):
                    last = pe.transpose(dst[:, j * P:(j + 1) * P], src[:, j, :], ident[:])
                last.then_inc(y_turned, 1)

            def turn_tile(n):
                pe.wait_ge(tile_unit, begun(n))
                pe.transpose(misc[:, 0:P], unit_t[:], ident[:]).then_inc(tile_turned, 1)

            pe.wait_ge(consts_ready, 3)
            pe.wait_ge(moments0_done, 1)
            for _ in range(WARM_UP):
                pe.transpose(misc[:, 0:P], ones[:], ident[:])
            pe.wait_ge(y_unit_dve, 1)
            turn_batch(y_unit0[:, 0:UNROLL, :], sums[0])
            pe.wait_ge(unit0_dve, X0_HALF)
            for t in range(X0_HALF):
                last = pe.transpose(scores[0][:, t * P:(t + 1) * P], unit0[:, t, :], ident[:])
            last.then_inc(turned0, 1)
            pe.wait_ge(unit0_dve, X0_UNIT_DVE)
            pe.wait_ge(unit0_act, X0 - X0_UNIT_DVE)
            for t in range(X0_HALF, CHUNK_TILES):
                pe.transpose(scores[0][:, t * P:(t + 1) * P], unit0[:, t, :], ident[:])
            pe.transpose(sums[2][:, 0:P], unit0[:, CHUNK_TILES, :], ident[:]).then_inc(turned0, 1)
            pe.wait_ge(y_split, 1)
            for h in range(CW // BANK):
                pe.wait_ge(split0, h + 1)
                for lhs, part in PRODUCTS:
                    last = half_score(scores[0], 0, 0, lhs, part, h)
            last.then_inc(scores_ready, 1)
            pe.wait_ge(y_unit_pool, 1)
            turn_batch(y_unit_b, misc)
            score(1, 1)
            pe.wait_ge(ymax_step, 1)
            pe.matmul(sums[1][0:1, 0:P], ymax_p[:], ident[:], start=True, stop=True).then_inc(ymax_moved, 1)
            pe.wait_ge(ymax_step, 2)
            pe.matmul(sums[1][:, P:P + 1], ones[0:1, :], ymax_1[:], start=True, stop=True).then_inc(ymax_moved, 1)

            def round_(c, r, first_round=False, first_chunk=False, y_prep=False, last_chunk=False, last_round=False):
                k = c * ROUNDS + r
                for u in range(UNROLL):
                    i = c * MT + (r * UNROLL + u)
                    if first_round and first_chunk and u == 2:
                        pe.wait_ge(y_split, Y_AHEAD)
                    elif u == 2 and not last_chunk:
                        pe.wait_ge(tile_split, begun(k + X_AHEAD - 2))
                    if not (last_round and u >= UNROLL - 2):
                        pe.wait_ge(exp_ready, i + 1)
                        score(i + 2, u)
                    if u == 0 and y_prep:
                        pe.wait_ge(y_unit_pool, r + Y_AHEAD)
                        if first_round and first_chunk:
                            pe.wait_ge(y_split, Y_AHEAD)
                        else:
                            pe.wait_ge(tile_split, begun(k + X_AHEAD - 2))
                        turn_batch(y_unit_b, misc)
                    if u == 2 and not last_chunk:
                        if y_prep:
                            pe.wait_ge(y_split, r + Y_AHEAD + 1)
                        elif first_round:
                            pe.wait_ge(total_done, 1)
                        turn_tile(k + X_AHEAD - 1)
                    if first_round and u == 0 and first_chunk:
                        continue
                    pe.wait_ge(lo_ready, i)
                    if u == 1 and first_chunk:
                        pe.wait_ge(v_ready, r + 1)
                    if u == 1 and first_round and first_chunk:
                        pe.wait_ge(ymax_done, 1)
                        pe.wait_ge(split0, 3)
                    last = add_values((r * UNROLL + (u - 1)) % MT, (u - 1) % UNROLL, first_round and u == 1,
                                      first_round and u == 0, c if not first_chunk else None)
                    if u == 0:
                        last.then_inc(round_summed, 1)

            def total_of_y():
                pe.wait_ge(folded, BATCHES + 1 + FOLDS)
                pe.wait_ge(tile_split, begun(ROUNDS - 1 + X_AHEAD - 1))
                pe.matmul(misc[:, 0:D], ones[:], fold[:, 0, :], start=True, stop=True).then_inc(total_summed, 1)

            sweep(pe, round_, total_of_y)
            pe.wait_ge(lo_ready, STEPS)
            add_values(MT - 1, UNROLL - 1, False, True, very_last=True)


def kernel(x, adj, L0_gnn_y):
    import concourse.bacc as bacc
    from concourse.bass_utils import run_bass_kernel_spmd

    x, adj, y = np.asarray(x), np.asarray(adj), np.asarray(L0_gnn_y)
    y_rows = y.reshape(P, MT, D)
    arrays = {
        "x": np.ascontiguousarray(x.reshape(P, NT, D)),
        "y": np.ascontiguousarray(y_rows),
        "adj_t": np.ascontiguousarray(
            adj.reshape(P, NC, CHUNK_TILES, P, MT).transpose(1, 4, 3, 2, 0).reshape(STEPS, P, CW)),
    }
    nc = bacc.Bacc("TRN2", target_bir_lowering=False, num_devices=1)
    aps = {name: nc.dram_tensor(name, a.shape, mybir.dt.from_np(a.dtype), kind="ExternalInput").ap()
           for name, a in arrays.items()}
    out = nc.dram_tensor("out", (P, NT, D), mybir.dt.float32, kind="ExternalOutput").ap()
    build(nc, aps["x"], aps["y"], aps["adj_t"], out)
    result = run_bass_kernel_spmd(nc, [arrays], core_ids=[0])
    return result.results[0]["out"].reshape(N, D)
```
